# Optimizing a Trainium2 kernel written in Bass

```python
import numpy as np
import jax
import jax.numpy as jnp

def _softmax(x, axis=-1):
    return jax.nn.softmax(x, axis=axis)

def _gelu(x):
    return jax.nn.gelu(x, approximate=True)

def _silu(x):
    return jax.nn.silu(x)

def _sigmoid(x):
    return jax.nn.sigmoid(x)

def _layernorm(x, axis=-1, eps=1e-05):
    m = jnp.mean(x, axis=axis, keepdims=True)
    v = jnp.var(x, axis=axis, keepdims=True)
    return (x - m) / jnp.sqrt(v + eps)

def _scatter_add(tgt, idx, src, axis=0):
    return tgt.at[idx].add(src)

def _segment_sum(src, seg, n):
    return jax.ops.segment_sum(src, seg, n)
kernel_name = 'mk_conv_preact_d2_conv_nchw512_r2_324dd7'

def setup_inputs(seed: int=0):
    np.random.seed(seed)
    _w = jnp.asarray

    def _rec_inputs():
        import jax
        import jax.numpy as jnp
        _gk = jax.random.key(seed)
        x = 7.22e-05 + 1 * jax.random.normal(jax.random.fold_in(_gk, 1), (4, 256, 32, 32), jnp.float32)
        return x
    x = _rec_inputs()

    def _L0_conv_setup():
        import jax, jax.numpy as jnp
        import numpy as np
        WS = 2
        DIM = 256
        NUM_HEADS = 8
        HEAD_DIM = DIM // NUM_HEADS
        L_HEADS = int(NUM_HEADS * 0.5)
        H_HEADS = NUM_HEADS - L_HEADS
        L_DIM = L_HEADS * HEAD_DIM
        H_DIM = H_HEADS * HEAD_DIM
        SCALE = HEAD_DIM ** (-0.5)
        key = jax.random.key(seed)
        ks = jax.random.split(key, 7)
        B, H, W = (4, 32, 32)
        s = 0.02
        return {'x': jax.random.normal(ks[0], (B, DIM, H, W), jnp.float32), 'h_qkv_w': jax.random.normal(ks[1], (DIM, 3 * H_DIM), jnp.float32) * s, 'h_proj_w': jax.random.normal(ks[2], (H_DIM, H_DIM), jnp.float32) * s, 'h_proj_b': jnp.zeros((H_DIM,), jnp.float32), 'l_q_w': jax.random.normal(ks[3], (DIM, L_DIM), jnp.float32) * s, 'l_kv_w': jax.random.normal(ks[4], (DIM, 2 * L_DIM), jnp.float32) * s, 'l_proj_w': jax.random.normal(ks[5], (L_DIM, L_DIM), jnp.float32) * s, 'l_proj_b': jnp.zeros((L_DIM,), jnp.float32)}
    _L0_conv_all = _L0_conv_setup()
    _L0_conv_in = {k: v for k, v in _L0_conv_all.items() if k in ('h_qkv_w', 'h_proj_w', 'h_proj_b', 'l_q_w', 'l_kv_w', 'l_proj_w', 'l_proj_b')}
    del _L0_conv_all

    def _L1_conv_setup():
        import jax, jax.numpy as jnp
        import numpy as np
        from jax import lax

        def _get_mu(x):
            bs, depth, h, w = x.shape
            ix = jnp.arange(1, h + 1, dtype=x.dtype).reshape(1, 1, h, 1)
            iy = jnp.arange(1, w + 1, dtype=x.dtype).reshape(1, 1, 1, w)
            sumX = jnp.maximum(x.sum((2, 3)), 1e-09)
            mu_x = jnp.maximum(jnp.round((ix * x).sum((2, 3)) / sumX), 1.0)
            mu_y = jnp.maximum(jnp.round((iy * x).sum((2, 3)) / sumX), 1.0)
            lin = jnp.linspace(-1.0, 1.0, h, dtype=x.dtype)
            mu_xg = lin[(mu_x - 1.0).astype(jnp.int32)]
            mu_yg = lin[(mu_y - 1.0).astype(jnp.int32)]
            return (mu_xg, mu_yg)

        def _get_mask(x, mask_weight, filt):
            bs, depth, h, w = x.shape
            mu_x, mu_y = _get_mu(x)
            posX = jnp.linspace(-1.0, 1.0, h, dtype=x.dtype).reshape(1, 1, h, 1)
            posY = jnp.linspace(-1.0, 1.0, w, dtype=x.dtype).reshape(1, 1, 1, w)
            m = jnp.abs(posX - mu_x[:, :, None, None]) + jnp.abs(posY - mu_y[:, :, None, None])
            m = 1.0 - m * mask_weight.reshape(1, depth, 1, 1)
            m = jnp.maximum(m, -1.0)
            m = jnp.where(filt.reshape(1, depth, 1, 1) == 1.0, m, 1.0)
            return m
        key = jax.random.key(seed)
        k1, k2, k3, k4 = jax.random.split(key, 4)
        bs, depth, h, w = (32, 256, 28, 28)
        out_c, kh, kw = (256, 3, 3)
        x = jax.random.uniform(k1, (bs, depth, h, w), dtype=jnp.float32)
        weight = jax.random.normal(k2, (out_c, depth, kh, kw), dtype=jnp.float32) * 0.02
        bias = jax.random.normal(k3, (out_c,), dtype=jnp.float32) * 0.02
        mask_weight = jax.random.uniform(k4, (depth,), dtype=jnp.float32)
        filt = jnp.ones((depth, 1), dtype=jnp.float32)
        return {'x': x, 'weight': weight, 'bias': bias, 'mask_weight': mask_weight, 'filter': filt, 'padding': 1}
    _L1_conv_all = _L1_conv_setup()
    _L1_conv_in = {k: v for k, v in _L1_conv_all.items() if k in ('weight', 'bias', 'mask_weight', 'filter')}
    del _L1_conv_all
    return {'x': x, 'L0_conv_h_qkv_w': _L0_conv_in['h_qkv_w'], 'L0_conv_h_proj_w': _L0_conv_in['h_proj_w'], 'L0_conv_h_proj_b': _L0_conv_in['h_proj_b'], 'L0_conv_l_q_w': _L0_conv_in['l_q_w'], 'L0_conv_l_kv_w': _L0_conv_in['l_kv_w'], 'L0_conv_l_proj_w': _L0_conv_in['l_proj_w'], 'L0_conv_l_proj_b': _L0_conv_in['l_proj_b'], 'L1_conv_weight': _L1_conv_in['weight'], 'L1_conv_bias': _L1_conv_in['bias'], 'L1_conv_mask_weight': _L1_conv_in['mask_weight'], 'L1_conv_filter': _L1_conv_in['filter']}

def reference(x, L0_conv_h_qkv_w, L0_conv_h_proj_w, L0_conv_h_proj_b, L0_conv_l_q_w, L0_conv_l_kv_w, L0_conv_l_proj_w, L0_conv_l_proj_b, L1_conv_weight, L1_conv_bias, L1_conv_mask_weight, L1_conv_filter):
    import jax
    import jax.numpy as jnp

    def _L0_conv_ref(x, h_qkv_w, h_proj_w, h_proj_b, l_q_w, l_kv_w, l_proj_w, l_proj_b):
        import jax, jax.numpy as jnp
        import numpy as np
        WS = 2
        DIM = 256
        NUM_HEADS = 8
        HEAD_DIM = DIM // NUM_HEADS
        L_HEADS = int(NUM_HEADS * 0.5)
        H_HEADS = NUM_HEADS - L_HEADS
        L_DIM = L_HEADS * HEAD_DIM
        H_DIM = H_HEADS * HEAD_DIM
        SCALE = HEAD_DIM ** (-0.5)
        B, C, H, W = x.shape
        xh = jnp.transpose(x, (0, 2, 3, 1))
        hg, wg = (H // WS, W // WS)
        G, N = (hg * wg, WS * WS)
        xw = xh.reshape(B, hg, WS, wg, WS, C).transpose(0, 1, 3, 2, 4, 5).reshape(B, G, N, C)
        qkv = (xw @ h_qkv_w).reshape(B, G, N, 3, H_HEADS, HEAD_DIM)
        qkv = jnp.transpose(qkv, (3, 0, 1, 4, 2, 5))
        q, k, v = (qkv[0], qkv[1], qkv[2])
        attn = jax.nn.softmax(jnp.einsum('bghnd,bghmd->bghnm', q, k) * SCALE, axis=-1)
        out = jnp.einsum('bghnm,bghmd->bghnd', attn, v)
        out = out.transpose(0, 1, 3, 2, 4).reshape(B, hg, wg, WS, WS, H_DIM)
        out = out.transpose(0, 1, 3, 2, 4, 5).reshape(B, H, W, H_DIM)
        hifi = out @ h_proj_w + h_proj_b
        q = (xh.reshape(B, H * W, C) @ l_q_w).reshape(B, H * W, L_HEADS, HEAD_DIM)
        pooled = xh.reshape(B, hg, WS, wg, WS, C).mean(axis=(2, 4)).reshape(B, G, C)
        kv = (pooled @ l_kv_w).reshape(B, G, 2, L_HEADS, HEAD_DIM)
        k, v = (kv[:, :, 0], kv[:, :, 1])
        attn = jax.nn.softmax(jnp.einsum('bnhd,bmhd->bhnm', q, k) * SCALE, axis=-1)
        lo = jnp.einsum('bhnm,bmhd->bnhd', attn, v).reshape(B, H * W, L_DIM)
        lofi = (lo @ l_proj_w + l_proj_b).reshape(B, H, W, L_DIM)
        out = jnp.concatenate([hifi, lofi], axis=-1)
        return jnp.transpose(out, (0, 3, 1, 2))

    def _L1_conv_ref(x, weight, bias, mask_weight, filter, padding):
        import jax, jax.numpy as jnp
        import numpy as np
        from jax import lax

        def _get_mu(x):
            bs, depth, h, w = x.shape
            ix = jnp.arange(1, h + 1, dtype=x.dtype).reshape(1, 1, h, 1)
            iy = jnp.arange(1, w + 1, dtype=x.dtype).reshape(1, 1, 1, w)
            sumX = jnp.maximum(x.sum((2, 3)), 1e-09)
            mu_x = jnp.maximum(jnp.round((ix * x).sum((2, 3)) / sumX), 1.0)
            mu_y = jnp.maximum(jnp.round((iy * x).sum((2, 3)) / sumX), 1.0)
            lin = jnp.linspace(-1.0, 1.0, h, dtype=x.dtype)
            mu_xg = lin[(mu_x - 1.0).astype(jnp.int32)]
            mu_yg = lin[(mu_y - 1.0).astype(jnp.int32)]
            return (mu_xg, mu_yg)

        def _get_mask(x, mask_weight, filt):
            bs, depth, h, w = x.shape
            mu_x, mu_y = _get_mu(x)
            posX = jnp.linspace(-1.0, 1.0, h, dtype=x.dtype).reshape(1, 1, h, 1)
            posY = jnp.linspace(-1.0, 1.0, w, dtype=x.dtype).reshape(1, 1, 1, w)
            m = jnp.abs(posX - mu_x[:, :, None, None]) + jnp.abs(posY - mu_y[:, :, None, None])
            m = 1.0 - m * mask_weight.reshape(1, depth, 1, 1)
            m = jnp.maximum(m, -1.0)
            m = jnp.where(filt.reshape(1, depth, 1, 1) == 1.0, m, 1.0)
            return m
        mask = _get_mask(x, mask_weight, filter)
        x_relu = jnp.maximum(x * mask, 0.0)
        out = lax.conv_general_dilated(x_relu, weight, window_strides=(1, 1), padding=[(padding, padding), (padding, padding)], dimension_numbers=('NCHW', 'OIHW', 'NCHW'))
        return out + bias.reshape(1, -1, 1, 1)

    def _gn(v, G=32, eps=1e-05):
        B_, C_, H_, W_ = v.shape
        g = v.reshape(B_, G, C_ // G, H_, W_)
        m = jnp.mean(g, axis=(2, 3, 4), keepdims=True)
        s = jnp.var(g, axis=(2, 3, 4), keepdims=True)
        return ((g - m) / jnp.sqrt(s + eps)).reshape(v.shape)

    def _ln_c(v, eps=1e-06):
        m = jnp.mean(v, axis=1, keepdims=True)
        s = jnp.var(v, axis=1, keepdims=True)
        return (v - m) / jnp.sqrt(s + eps)

    def _ln_t(v, eps=1e-05):
        m = jnp.mean(v, axis=-1, keepdims=True)
        s = jnp.var(v, axis=-1, keepdims=True)
        return (v - m) / jnp.sqrt(s + eps)

    def _to_tokens(v):
        B_, C_, H_, W_ = v.shape
        return v.reshape(B_, C_, H_ * W_).transpose(0, 2, 1)

    def _from_tokens(t, like):
        B_, C_, H_, W_ = like.shape
        return t.transpose(0, 2, 1).reshape(B_, C_, H_, W_)
    x = x + _L0_conv_ref(_gn(x), L0_conv_h_qkv_w, L0_conv_h_proj_w, L0_conv_h_proj_b, L0_conv_l_q_w, L0_conv_l_kv_w, L0_conv_l_proj_w, L0_conv_l_proj_b)
    x = x + _L1_conv_ref(_gn(x), L1_conv_weight, L1_conv_bias, L1_conv_mask_weight, L1_conv_filter, 1)
    return x

_drawn_inputs = setup_inputs


def setup_inputs(seed=0):
    import zlib

    import numpy as np

    out = dict(_drawn_inputs(seed))
    spreads = {'L0_conv_h_proj_b': (0.0, 0.1),
     'L0_conv_l_proj_b': (0.0, 0.1),
     'L1_conv_filter': (1.0, 0.2)}
    factors = {'L0_conv_l_q_w': 8.0,
     'L0_conv_l_kv_w': 8.0,
     'L0_conv_l_proj_w': 8.0,
     'L1_conv_bias': 3.315,
     'L0_conv_h_qkv_w': 2.684,
     'L0_conv_h_proj_w': 2.679}
    for name, (base, spread) in spreads.items():
        noise = np.random.default_rng([zlib.crc32(name.encode()), seed]).standard_normal(out[name].shape)
        drawn = base * np.exp(spread * noise) if base else spread * noise
        out[name] = jnp.asarray(drawn.astype(out[name].dtype))
    for name, factor in factors.items():
        out[name] = (out[name] * factor).astype(out[name].dtype)
    return out
```

```python
from contextlib import ExitStack

import concourse.bass as bass
from concourse import mybir

F32 = mybir.dt.float32
F32R = mybir.dt.float32r
I32 = mybir.dt.int32
ALU = mybir.AluOpType
ACT = mybir.ActivationFunctionType
AX_X = mybir.AxisListType.X

P = 128
B, C, H, W = 4, 256, 32, 32
KT = C // P
HW = H * W
WS = 2
NW = WS * WS
HG, WG = H // WS, W // WS
G = HG * WG
HALF = 512
HEADS, HD = 4, 32
SCALE = HD ** -0.5
MT = G // P
LT = HEADS * MT
NB = HW // P
TAPS = 9
PADW = W + 2
GROUP = 8
EPS = 1e-5
ROUND = 12582912.0
MAGIC = 0x5F3759DF
IX_SUM = float(W * H * (H + 1) // 2)
LIN = 2.0 / (H - 1)

C_ID, C_GRP, C_HEAD, C_ONE = 0, P, 2 * P, 2 * P + HD
C_BLK = C_ONE + HD
C_IX = C_BLK + NB
C_POS = C_IX + H
C_ALL = C_POS + H
SEL_COLS = (HEADS + NW) * P

WQ, WK, WV, WLQ, WLK, WLV = (P * i for i in range(6))
WCOLS = 6 * P

LA_SLOT = (0, 1, 2, 0, 1, 2, 0, 1)
ST_SLOT = (0, 1, 0, 1, 1, 2, 0, 1)
PB_SLOT = (0, 1, 2, 0)

GROUPS = 2 * KT
CONV_MM = KT * TAPS * 3

N_GN, N_MASK, N_SOFT, N_POOL = 20, 17, 5, 4
GN_SENT, SOFT_READ = 4, 2


def wait_count(eng, sem, n):
    if not (isinstance(n, int) and n <= 0):
        eng.wait_ge(sem, n)


class Chain:

    def __init__(self, eng, sem, length, image):
        self.eng, self.sem, self.base, self.length, self.n = eng, sem, image * length, length, 0

    def __call__(self, ins):
        self.n += 1
        ins.then_inc(self.sem, 1)
        if self.n < self.length:
            self.eng.wait_ge(self.sem, self.base + self.n)


def build(nc, x, wqkv, whp, wlp, bh, bl, cw, cb, mw, filt, consts, selectors, out):
    with ExitStack() as ctx:
        def sb(name, shape, dt=F32):
            return ctx.enter_context(nc.sbuf_tensor(name, shape, dt))

        def sem(name):
            return ctx.enter_context(nc.semaphore(name))

        xy = sb("xy", [P, B * KT * HW])
        cst = sb("cst", [P, C_ALL])
        sel = sb("sel", [P, HEADS + NW, P], F32R)
        w_hi = sb("w_hi", [P, KT, WCOLS], F32R)
        w_lo = sb("w_lo", [P, KT, WCOLS], F32R)
        w_out = sb("w_out", [P, 2, P])
        bias = sb("bias", [P, 2])
        cw_hi = sb("cw_hi", [P, KT * TAPS * C], F32R)
        cw_lo = sb("cw_lo", [P, KT * TAPS * C], F32R)
        cbias = sb("cbias", [P, KT])
        mwf = sb("mwf", [P, 3, KT])
        xn = sb("xn", [P, KT, HW])
        xn_hi = sb("xn_hi", [P, KT, HW], F32R)
        xn_lo = sb("xn_lo", [P, KT, HW], F32R)
        p_hi, p_lo = xn_hi[:, 0], xn_lo[:, 0]
        pool_hi = sb("pool_hi", [P, KT, G], F32R)
        pool_lo = sb("pool_lo", [P, KT, G], F32R)
        q_w = sb("q_w", [P, HW])
        k_w = sb("k_w", [P, HW])
        v_w = sb("v_w", [P, HW])
        lq_hi = sb("lq_hi", [P, HW], F32R)
        lq_lo = sb("lq_lo", [P, HW], F32R)
        lk_hi = sb("lk_hi", [P, HEADS, G], F32R)
        lk_lo = sb("lk_lo", [P, HEADS, G], F32R)
        lv = sb("lv", [P, MT, P])
        probs = sb("probs", [P, LT, HW])
        qk = probs[:, LT - NW:LT, :]
        raw = probs[:].rearrange("p a b -> p (a b)")
        raw_cw = raw[:, 0:KT * TAPS * C]
        raw_sel = raw[:, raw.shape[1] - SEL_COLS:]
        raw_w = raw[:, KT * TAPS * C:KT * TAPS * C + KT * WCOLS].rearrange("p (k n) -> p k n", k=KT)
        s_soft = sb("s_soft", [P, NB, NW, HD])
        s_max = sb("s_max", [P, NB, HEADS])
        s_den = sb("s_den", [P, NB, HEADS])
        l_max = sb("l_max", [P, P])
        l_rows = xn_hi[:, 1].rearrange("p (n t) -> p n t", n=NB)
        im_hi = sb("im_hi", [P, KT, PADW * PADW], F32R)
        im_lo = sb("im_lo", [P, KT, PADW * PADW], F32R)
        mask = sb("mask", [P, KT, HW])
        pool_t, pool_s = mask[:, :, 0:2 * G], mask[:, :, 2 * G:3 * G]
        st = [sb(f"st{i}", [P, KT, 2, 6]) for i in range(2)]
        mv = [sb(f"mv{i}", [P, KT, 2]) for i in range(2)]
        gn = [sb(f"gn{i}", [P, 8, KT]) for i in range(2)]
        rc = sb("rc", [P, KT, 2, H])
        rw = sb("rw", [P, KT, 2, H])
        mu = sb("mu", [P, KT, 2])
        sx = gn[1][:, 2:4]

        cps = ctx.enter_context(nc.psum_tensor("cps", [P, 2, HALF], F32))
        slot = [ctx.enter_context(nc.psum_tensor(f"slot{i}", [P, 2, HALF], F32)) for i in range(3)]
        flat = [s[:].rearrange("p a b -> p (a b)") for s in slot]

        x_in = [sem(f"x_in{b}") for b in range(B)]
        w_in, cw_in, c_in = sem("w_in"), sem("cw_in"), sem("c_in")
        out_done = sem("out_done")
        w_ready = sem("w_ready")
        cw_split = sem("cw_split")
        zeroed = sem("zeroed")
        zeroed_dve = sem("zeroed_dve")
        gn_c = [sem("gn1_c"), sem("gn2_c")]
        gn_pe = [sem("gn1_pe"), sem("gn2_pe")]
        mask_c, soft_c, pool_c = sem("mask_c"), sem("soft_c"), sem("pool_c")
        xhi_ready, xn_ready = sem("xhi_ready"), sem("xn_ready")
        xlo_ready = sem("xlo_ready")
        proj_pe = sem("proj_pe")
        qkv_sb = sem("qkv_sb")
        lq_act, lq_dve = sem("lq_act"), sem("lq_dve")
        lk_act, lk_dve = sem("lk_act"), sem("lk_dve")
        prod_ready = sem("prod_ready")
        ssum_pe, ssum_sb = sem("ssum_pe"), sem("ssum_sb")
        stok_pe, sexp = sem("stok_pe"), sem("sexp")
        pt_pe, pt_act, pt_dve = sem("pt_pe"), sem("pt_act"), sem("pt_dve")
        la_pe, la_max = sem("la_pe"), sem("la_max")
        lmt_pe, lrows = sem("lmt_pe"), sem("lrows")
        pb_pe, pv_ready = sem("pb_pe"), sem("pv_ready")
        pv_pool, pv_dve = sem("pv_pool"), sem("pv_dve")
        st_pe, st_exp = sem("st_pe"), sem("st_exp")
        lden_pe, lden_dve = sem("lden_pe"), sem("lden_dve")
        lpv_pe, lnorm = sem("lpv_pe"), sem("lnorm")
        out_pe, y_ready = sem("out_pe"), sem("y_ready")
        yn_ready = sem("yn_ready")
        msum, masked = sem("msum"), sem("masked")
        im_act, im_dve = sem("im_act"), sem("im_dve")
        conv_pe, conv_out = sem("conv_pe"), sem("conv_out")

        block = ctx.enter_context(nc.Block())

        def img(b, k, lo=0, n=HW):
            return xy[:, bass.ds(b * (KT * HW) + (k * HW + lo), n)]

        def run(eng, step):
            step(0, True, False)
            with eng.Fori(1, B - 1) as b:
                step(b, False, False)
            step(B - 1, False, True)

        @block.sync
        def _(sp):
            for b in range(B):
                for k in range(KT):
                    sp.dma_start(img(b, k), x[b, k]).then_inc(x_in[b], 16)
                if b == 0:
                    sp.dma_start(cst[:], consts).then_inc(c_in, 16)
                    sp.dma_start(raw_sel, selectors).then_inc(c_in, 16)
                    for c0, src in zip((WQ, WLQ, WLK), wqkv):
                        for k in range(KT):
                            sp.dma_start(raw_w[:, k, c0:c0 + src.shape[2]], src[k]).then_inc(w_in, 16)
                    for dst, src in ((w_out[:, 0], whp), (w_out[:, 1], wlp), (bias[:, 0:1], bh), (bias[:, 1:2], bl),
                                     (cbias[:], cb), (mwf[:, 0], mw), (mwf[:, 1], filt)):
                        sp.dma_start(dst, src).then_inc(c_in, 16)
                    for k in range(KT):
                        sp.dma_start(raw_cw[:, k * TAPS * C:(k + 1) * TAPS * C], cw[k]).then_inc(cw_in, 16)
            with sp.Fori(0, B) as b:
                for o in range(KT):
                    sp.wait_ge(conv_out, b * GROUPS + 2 * (o + 1))
                    sp.dma_start(out[bass.ds(b, 1), o].rearrange("b p n -> p (b n)"), img(b, o)).then_inc(out_done, 16)
            sp.wait_ge(out_done, B * KT * 16)

        CONST_LOADS = 9 * 16

        @block.gpsimd
        def _(pool):
            def mask_sum(b, pooled):
                pool.wait_ge(mask_c, (b + 1) * N_MASK)
                pool.wait_ge(pool_c, pooled * N_POOL)
                for k in range(KT):
                    nc.gpsimd.tensor_tensor(mask[:, k].rearrange("p (h w) -> p h w", h=H),
                                            rw[:, k, 0].unsqueeze(2).to_broadcast([P, H, W]),
                                            rw[:, k, 1].unsqueeze(1).to_broadcast([P, H, W]),
                                            ALU.add).then_inc(msum, 1)

            def products(b, keys):
                for j in keys:
                    nc.gpsimd.tensor_tensor(
                        qk[:, j].rearrange("p (n w) -> p n w", n=NW),
                        q_w[:].rearrange("p (n w) -> p n w", n=NW),
                        k_w[:, j * G:(j + 1) * G].unsqueeze(1).to_broadcast([P, NW, G]),
                        ALU.mult).then_inc(prod_ready, 1)

            def step(b, first, last):
                pool.wait_ge(qkv_sb, b * 3 + 2)
                wait_count(pool, lpv_pe, b)
                products(b, (0, 1))
                if not first:
                    mask_sum(b - 1, b + 1)
                products(b, (2, 3))
                for j in (0, 2):
                    pool.wait_ge(pv_ready, b * NW + j + 2)
                    nc.gpsimd.tensor_tensor(qk[:, j], qk[:, j], qk[:, j + 1], ALU.add).then_inc(pv_pool, 1)

            for t in (lk_hi, lk_lo, im_hi, im_lo):
                nc.gpsimd.memset(t[:].bitcast(F32), 0.0).then_inc(zeroed, 1)
            pool.wait_ge(cw_in, KT * 16)
            nc.gpsimd.tensor_scalar(cw_hi[:], raw_cw, 1.0, 0.0, ALU.mult, ALU.add).then_inc(cw_split, 1)
            pool.wait_ge(cw_split, 1)
            nc.gpsimd.tensor_tensor(cw_lo[:], raw_cw, cw_hi[:].bitcast(F32), ALU.subtract).then_inc(cw_split, 1)
            pool.wait_ge(cw_split, 2)
            pool.wait_ge(w_ready, 3)
            run(pool, step)
            mask_sum(B - 1, B)

        @block.scalar
        def _(act):
            def normalise(b):
                act.wait_ge(gn_c[0], (b + 1) * N_GN)
                wait_count(act, pb_pe, b * NW)
                wait_count(act, xlo_ready, b * KT)
                wait_count(act, pool_c, b * N_POOL)
                for k in range(KT):
                    src = img(b, k).rearrange("p (hg a wg b) -> p a b hg wg", hg=HG, a=WS, wg=WG, b=WS)
                    for t, ready in ((xn_hi, xhi_ready), (xn, xn_ready)):
                        dst = t[:, k].rearrange("p (a b hg wg) -> p a b hg wg", a=WS, b=WS, hg=HG)
                        for a in range(WS):
                            last = nc.scalar.activation(dst[:, a], src[:, a], ACT.Identity,
                                                        bias=gn[0][:, 6, k:k + 1], scale=gn[0][:, 5, k:k + 1])
                        last.then_inc(ready, 1)

            def projections(b):
                wait_count(act, y_ready, b * KT)
                for i, dst in enumerate((q_w, k_w, v_w)):
                    act.wait_ge(proj_pe, b * 5 + i + 1)
                    nc.scalar.copy(dst[:], flat[i]).then_inc(qkv_sb, 1)
                act.wait_ge(proj_pe, b * 5 + 4)
                nc.scalar.copy(lq_hi[:], flat[0]).then_inc(lq_act, 1)
                act.wait_ge(proj_pe, b * 5 + 5)
                for h in range(HEADS):
                    r = slice(HD * h, HD * (h + 1))
                    nc.scalar.copy(lk_hi[r, h], slot[1][r, 0, 0:G]).then_inc(lk_act, 1)
                nc.scalar.activation(lv[:].rearrange("p a b -> p (a b)"), slot[1][:, 1, 0:MT * P], ACT.Copy,
                                     scale=1.0 / NW).then_inc(lk_act, 1)

            def conv_input(b, normalised):
                act.wait_ge(gn_c[1], (b + 1) * N_GN)
                act.wait_ge(xlo_ready, normalised * KT)
                act.wait_ge(pool_c, normalised * N_POOL)
                for k in range(KT):
                    nc.scalar.activation(xn[:, k], img(b, k), ACT.Identity, bias=gn[1][:, 6, k:k + 1],
                                         scale=gn[1][:, 5, k:k + 1]).then_inc(yn_ready, 1)
                wait_count(act, conv_pe, b * GROUPS)
                for k in range(KT):
                    act.wait_ge(masked, b * KT + k + 1)
                    inner = im_hi[:, k].rearrange("p (h w) -> p h w", h=PADW)[:, 1:H + 1, 1:W + 1]
                    nc.scalar.activation(inner, mask[:, k].rearrange("p (h w) -> p h w", h=H),
                                         ACT.Relu).then_inc(im_act, 1)

            def exp_scores(b, tiles):
                for i in tiles:
                    act.wait_ge(st_pe, b * LT + i + 1)
                    nc.scalar.activation(probs[:, i], flat[ST_SLOT[i]], ACT.Exp, scale=SCALE / NW)\
                        .then_inc(st_exp, 1)

            def step(b, first, last):
                if first:
                    normalise(b)
                    act.wait_ge(zeroed, 4)
                    act.wait_ge(w_ready, 3)
                    act.wait_ge(cw_split, 2)
                projections(b)
                if not first:
                    conv_input(b - 1, b + 1)
                act.wait_ge(ssum_pe, b + 1)
                nc.scalar.copy(q_w[:], flat[0]).then_inc(ssum_sb, 1)
                act.wait_ge(soft_c, b * N_SOFT + SOFT_READ)
                nc.scalar.activation(s_soft[:, :, :, 0:HEADS], s_soft[:, :, :, 0:HEADS], ACT.Exp,
                                     scale=SCALE).then_inc(sexp, 1)
                exp_scores(b, range(LT - NW))
                act.wait_ge(pt_pe, b + 1)
                nc.scalar.copy(p_hi, flat[2]).then_inc(pt_act, 1)
                act.wait_ge(pv_dve, b + 1)
                exp_scores(b, range(LT - NW, LT))
                if not last:
                    normalise(b + 1)

            run(act, step)
            conv_input(B - 1, B)

        @block.vector
        def _(dve):
            def statistics(b, i):
                link = Chain(dve, gn_c[i], N_GN, b)
                s, m, g = st[i], mv[i], gn[i]
                for k in range(KT):
                    for half in range(2):
                        last = nc.vector.bn_stats(s[:, k, half], img(b, k, half * HALF, HALF))
                link(last)
                nc.vector.memset(g[:, 7], 0.0)
                for k in range(KT):
                    last = nc.vector.bn_aggr(m[:, k], s[:, k].rearrange("p a b -> p (a b)"))
                link(last)
                link(nc.vector.tensor_tensor(g[:, 2], m[:, :, 0], m[:, :, 0], ALU.mult))
                link(nc.vector.tensor_tensor(m[:, :, 1], m[:, :, 1], g[:, 2], ALU.add))
                dve.wait_ge(gn_pe[i], b + 1)
                src = slot[1 + i][:, 0, 0:2 * KT].rearrange("p (k s) -> p s k", s=2)
                link(nc.vector.tensor_copy(g[:, 0:2], src))
                link(nc.vector.tensor_tensor(g[:, 2], g[:, 0], g[:, 0], ALU.mult))
                link(nc.vector.scalar_tensor_tensor(g[:, 3], g[:, 1], EPS, g[:, 2], ALU.add, ALU.subtract))
                link(nc.vector.tensor_scalar(g[:, 4], g[:, 3], -0.5, None, ALU.mult))
                link(nc.vector.tensor_scalar(g[:, 7].bitcast(I32), g[:, 3].bitcast(I32), 1, None,
                                             ALU.logical_shift_right))
                link(nc.vector.tensor_scalar(g[:, 5].bitcast(I32), g[:, 7].bitcast(I32), -1.0, float(MAGIC),
                                             ALU.mult, ALU.add))
                for _ in range(3):
                    link(nc.vector.tensor_tensor(g[:, 7], g[:, 5], g[:, 5], ALU.mult))
                    link(nc.vector.tensor_tensor(g[:, 7], g[:, 7], g[:, 4], ALU.mult))
                    link(nc.vector.scalar_tensor_tensor(g[:, 5], g[:, 7], 1.5, g[:, 5], ALU.add, ALU.mult))
                link(nc.vector.scalar_tensor_tensor(g[:, 6], g[:, 0], -1.0, g[:, 5], ALU.mult, ALU.mult))
                assert link.n == N_GN

            def split_input(b):
                wait_count(dve, proj_pe, b * 5)
                for k in range(KT):
                    dve.wait_ge(xhi_ready, b * KT + k + 1)
                    dve.wait_ge(xn_ready, b * KT + k + 1)
                    nc.vector.tensor_tensor(xn_lo[:, k], xn[:, k], xn_hi[:, k].bitcast(F32),
                                            ALU.subtract).then_inc(xlo_ready, 1)
                link = Chain(dve, pool_c, N_POOL, b)
                link(nc.vector.tensor_tensor(pool_t, xn[:, :, 0:2 * G], xn[:, :, 2 * G:4 * G], ALU.add))
                link(nc.vector.tensor_tensor(pool_s, pool_t[:, :, 0:G], pool_t[:, :, G:2 * G], ALU.add))
                link(nc.vector.tensor_copy(pool_hi[:], pool_s))
                link(nc.vector.tensor_tensor(pool_lo[:], pool_s, pool_hi[:].bitcast(F32), ALU.subtract))

            def mask_parts(b):
                link = Chain(dve, mask_c, N_MASK, b)
                g = gn[1]
                y = xy[:, bass.ds(b * (KT * HW), KT * HW)]
                nc.vector.tensor_reduce(rc[:, :, 0], y.rearrange("p (k h w) -> p k h w", k=KT, h=H), AX_X, ALU.add)
                link(nc.vector.tensor_reduce(rc[:, :, 1], y.rearrange("p (k h w) -> p k w h", k=KT, h=H), AX_X, ALU.add))
                both = [t[:].rearrange("p k s n -> p (k s) n") for t in (rc, rw)]
                m4 = mu[:].rearrange("p k s -> p (k s)")
                link(nc.vector.tensor_tensor(both[1], both[0],
                                             cst[:, C_IX:C_IX + H].unsqueeze(1).to_broadcast([P, 2 * KT, H]), ALU.mult))
                link(nc.vector.tensor_reduce(m4, both[1], AX_X, ALU.add))
                link(nc.vector.tensor_tensor(sx[:, 0], mv[1][:, :, 0], g[:, 0], ALU.subtract))
                link(nc.vector.scalar_tensor_tensor(sx[:, 0], sx[:, 0], float(HW), g[:, 5], ALU.mult, ALU.mult))
                link(nc.vector.tensor_scalar(sx[:, 0], sx[:, 0], 1e-9, None, ALU.max))
                link(nc.vector.reciprocal(sx[:, 1], sx[:, 0]))
                link(nc.vector.tensor_tensor(sx[:, 1], sx[:, 1], g[:, 5], ALU.mult))
                link(nc.vector.scalar_tensor_tensor(mu[:], g[:, 0].unsqueeze(2).to_broadcast([P, KT, 2]), -IX_SUM,
                                                    mu[:], ALU.mult, ALU.add))
                link(nc.vector.tensor_tensor(mu[:], mu[:], sx[:, 1].unsqueeze(2).to_broadcast([P, KT, 2]), ALU.mult))
                link(nc.vector.tensor_scalar(m4, m4, 1.0, float(H), ALU.max, ALU.min))
                link(nc.vector.tensor_scalar(m4, m4, ROUND, -ROUND, ALU.add, ALU.add))
                link(nc.vector.tensor_scalar(m4, m4, LIN, -1.0 - LIN, ALU.mult, ALU.add))
                link(nc.vector.tensor_tensor(both[0], cst[:, C_POS:C_POS + H].unsqueeze(1).to_broadcast([P, 2 * KT, H]),
                                             m4.unsqueeze(2).to_broadcast([P, 2 * KT, H]), ALU.subtract))
                link(nc.vector.scalar_tensor_tensor(both[1], both[0], -1.0, both[0], ALU.mult, ALU.max))
                link(nc.vector.tensor_tensor(rw[:].rearrange("p k s n -> p k (s n)"),
                                             rw[:].rearrange("p k s n -> p k (s n)"),
                                             mwf[:, 2].unsqueeze(2).to_broadcast([P, KT, 2 * H]), ALU.mult))
                link(nc.vector.tensor_scalar(rw[:, :, 0], rw[:, :, 0], 1.0, None, ALU.add))
                assert link.n == N_MASK

            def masked_image(b):
                for k in range(KT):
                    dve.wait_ge(msum, b * KT + k + 1)
                    dve.wait_ge(yn_ready, b * KT + k + 1)
                    nc.vector.scalar_tensor_tensor(mask[:, k], mask[:, k], -1.0, xn[:, k], ALU.max,
                                                   ALU.mult).then_inc(masked, 1)
                wait_count(dve, conv_pe, b * GROUPS)
                for k in range(KT):
                    dve.wait_ge(im_act, b * KT + k + 1)
                    inner = [t[:, k].rearrange("p (h w) -> p h w", h=PADW)[:, 1:H + 1, 1:W + 1] for t in (im_hi, im_lo)]
                    nc.vector.scalar_tensor_tensor(inner[1], mask[:, k].rearrange("p (h w) -> p h w", h=H), 0.0,
                                                   inner[0].bitcast(F32), ALU.max, ALU.subtract).then_inc(im_dve, 1)

            def pooled_lo(b):
                dve.wait_ge(lq_act, b + 1)
                nc.vector.tensor_tensor(lq_lo[:], flat[0], lq_hi[:].bitcast(F32), ALU.subtract).then_inc(lq_dve, 1)
                dve.wait_ge(lk_act, b * 5 + 5)
                for h in range(HEADS):
                    r = slice(HD * h, HD * (h + 1))
                    nc.vector.tensor_tensor(lk_lo[r, h], slot[1][r, 0, 0:G], lk_hi[r, h].bitcast(F32),
                                            ALU.subtract).then_inc(lk_dve, 1)

            def maxima(b):
                for n in range(NB):
                    dve.wait_ge(la_pe, b * NB + n + 1)
                    nc.vector.tensor_reduce(l_max[:, n * HEADS:(n + 1) * HEADS],
                                            flat[LA_SLOT[n]].rearrange("p (h m) -> p h m", h=HEADS), AX_X, ALU.max,
                                            negate=True).then_inc(la_max, 1)
                dve.wait_ge(lmt_pe, b + 1)
                nc.vector.tensor_tensor(l_rows[:], slot[2][:, 0, 0:P].unsqueeze(1).to_broadcast([P, NB, P]),
                                        cst[:, C_BLK:C_BLK + NB].unsqueeze(2).to_broadcast([P, NB, P]),
                                        ALU.mult).then_inc(lrows, 1)

            def window_softmax(b):
                link = Chain(dve, soft_c, N_SOFT, b)
                dve.wait_ge(stok_pe, b + 1)
                s = flat[2].rearrange("p (n j h) -> p n j h", n=NB, j=NW)[:, :, :, 0:HEADS]
                e = s_soft[:, :, :, 0:HEADS]
                link(nc.vector.tensor_reduce(s_max[:], s.rearrange("p n j h -> p n h j"), AX_X, ALU.max))
                link(nc.vector.tensor_tensor(e, s, s_max[:].unsqueeze(2).to_broadcast([P, NB, NW, HEADS]), ALU.subtract))
                dve.wait_ge(sexp, b + 1)
                link(nc.vector.tensor_reduce(s_den[:], e.rearrange("p n j h -> p n h j"), AX_X, ALU.add))
                link(nc.vector.reciprocal(s_max[:], s_den[:]))
                link(nc.vector.tensor_tensor(e, e, s_max[:].unsqueeze(2).to_broadcast([P, NB, NW, HEADS]), ALU.mult))

            def conv_result(b, groups):
                for g in groups:
                    o, half = divmod(g, 2)
                    dve.wait_ge(conv_pe, b * GROUPS + g + 1)
                    dst = img(b, o, half * HALF, HALF)
                    nc.vector.scalar_tensor_tensor(dst, cps[:, g % 2], cbias[:, o:o + 1], dst, ALU.add,
                                                   ALU.add).then_inc(conv_out, 1)

            def residual(b, k, s):
                dve.wait_ge(out_pe, b * 2 + k + 1)
                y = img(b, k).rearrange("p (hg a wg b) -> p a b hg wg", hg=HG, a=WS, wg=WG, b=WS)
                for n in range(NW):
                    dst = y[:, n // WS, n % WS]
                    last = nc.vector.scalar_tensor_tensor(
                        dst, flat[s][:, n * G:(n + 1) * G].rearrange("p (hg wg) -> p hg wg", hg=HG),
                        bias[:, k:k + 1], dst, ALU.add, ALU.add)
                last.then_inc(y_ready, 1)

            def step(b, first, last):
                if first:
                    dve.wait_ge(x_in[0], KT * 16)
                    statistics(b, 0)
                    split_input(b)
                else:
                    dve.wait_ge(y_ready, b * KT)
                    statistics(b - 1, 1)
                    mask_parts(b - 1)
                pooled_lo(b)
                if not first:
                    masked_image(b - 1)
                maxima(b)
                window_softmax(b)
                if not first:
                    conv_result(b - 1, (0,))
                dve.wait_ge(pt_act, b + 1)
                nc.vector.tensor_tensor(p_lo, flat[2], p_hi.bitcast(F32), ALU.subtract).then_inc(pt_dve, 1)
                for j in range(NW):
                    dve.wait_ge(pb_pe, b * NW + j + 1)
                    nc.vector.tensor_tensor(
                        qk[:, j].rearrange("p (n w) -> p n w", n=NW),
                        flat[PB_SLOT[j]].rearrange("p (n w) -> p n w", n=NW),
                        v_w[:, j * G:(j + 1) * G].unsqueeze(1).to_broadcast([P, NW, G]),
                        ALU.mult).then_inc(pv_ready, 1)
                if first:
                    for i in range(1, B):
                        dve.wait_ge(x_in[i], KT * 16)
                if not last:
                    statistics(b + 1, 0)
                dve.wait_ge(pv_pool, b * 2 + 2)
                nc.vector.tensor_tensor(q_w[:], qk[:, 0], qk[:, 2], ALU.add).then_inc(pv_dve, 1)
                if not first:
                    conv_result(b - 1, (1,))
                dve.wait_ge(lden_pe, b + 1)
                nc.vector.reciprocal(k_w[:], flat[2]).then_inc(lden_dve, 1)
                dve.wait_ge(lden_dve, b + 1)
                dve.wait_ge(lpv_pe, b + 1)
                nc.vector.tensor_tensor(k_w[:], flat[0], k_w[:], ALU.mult).then_inc(lnorm, 1)
                residual(b, 0, 1)
                if not first:
                    conv_result(b - 1, (2,))
                residual(b, 1, 2)
                if not last:
                    split_input(b + 1)
                if not first:
                    conv_result(b - 1, (3,))

            nc.vector.memset(s_soft[:], 0.0)
            nc.vector.memset(l_max[:], 0.0).then_inc(zeroed_dve, 1)
            dve.wait_ge(c_in, CONST_LOADS)
            nc.vector.tensor_copy(sel[:].rearrange("p a b -> p (a b)"), raw_sel).then_inc(w_ready, 1)
            dve.wait_ge(w_in, 3 * KT * 16)
            nc.vector.tensor_copy(w_hi[:], raw_w).then_inc(w_ready, 1)
            dve.wait_ge(w_ready, 2)
            nc.vector.tensor_tensor(w_lo[:], raw_w, w_hi[:].bitcast(F32), ALU.subtract).then_inc(w_ready, 1)
            nc.vector.scalar_tensor_tensor(mwf[:, 2], mwf[:, 1], 1.0, mwf[:, 0], ALU.is_equal,
                                           ALU.mult).then_inc(w_ready, 1)
            dve.wait_ge(w_ready, 4)
            nc.vector.tensor_scalar(mwf[:, 2], mwf[:, 2], -1.0, None, ALU.mult).then_inc(w_ready, 1)
            dve.wait_ge(w_ready, 5)
            run(dve, step)
            dve.wait_ge(y_ready, B * KT)
            statistics(B - 1, 1)
            mask_parts(B - 1)
            masked_image(B - 1)
            conv_result(B - 1, range(GROUPS))

        @block.tensor
        def _(pe):
            def mm(dst, lhsT, rhs, start, stop):
                return nc.tensor.matmul(dst, lhsT, rhs, start=start, stop=stop)

            def split_mm(dst, lhsT, rhs, start=True, stop=True):
                mm(dst, lhsT[0], rhs[0], start, False)
                mm(dst, lhsT[0], rhs[1], False, False)
                return mm(dst, lhsT[1], rhs[0], False, stop)

            def halves(i):
                return slice(i * HALF, (i + 1) * HALF)

            class Convolution:

                def __init__(self, b):
                    self.b, self.at = b, 0

                def more(self, n):
                    b = self.b
                    for i in range(self.at, min(self.at + n, GROUPS * CONV_MM)):
                        if i == 0:
                            pe.wait_ge(im_act, (b + 1) * KT)
                            pe.wait_ge(im_dve, (b + 1) * KT)
                        g, m = divmod(i, CONV_MM)
                        if m == 0 and g >= 2:
                            pe.wait_ge(conv_out, b * GROUPS + g - 1)
                        o, half = divmod(g, 2)
                        kt, part = divmod(m, 3)
                        k, tap = divmod(kt, TAPS)
                        dy, dx = divmod(tap, 3)
                        c0 = (k * TAPS + tap) * C + o * P
                        im = (im_hi, im_lo, im_hi)[part][:, k].rearrange("p (h w) -> p h w", h=PADW)
                        y0 = dy + half * (H // 2)
                        ins = mm(cps[:, g % 2].rearrange("p (h w) -> p h w", w=W),
                                 (cw_hi, cw_hi, cw_lo)[part][:, c0:c0 + P],
                                 im[:, y0:y0 + H // 2, dx:dx + W], m == 0, m == CONV_MM - 1)
                        if m == CONV_MM - 1:
                            ins.then_inc(conv_pe, 1)
                    self.at += n

            class NoConvolution:
                def more(self, n):
                    pass

            def group_means(b, i):
                pe.wait_ge(gn_c[i], b * N_GN + GN_SENT)
                mm(slot[1 + i][:, 0, 0:2 * KT], cst[:, C_GRP:C_GRP + P], mv[i][:].rearrange("p k s -> p (k s)"),
                   True, True).then_inc(gn_pe[i], 1)

            def project(s, c0):
                for i in range(2):
                    for k in range(KT):
                        last = split_mm(slot[s][:, i], (w_hi[:, k, c0:c0 + P], w_lo[:, k, c0:c0 + P]),
                                        (xn_hi[:, k, halves(i)], xn_lo[:, k, halves(i)]), k == 0, k == KT - 1)
                last.then_inc(proj_pe, 1)

            def pooled_scores(b, i):
                h, t = divmod(i, MT)
                s = slot[ST_SLOT[i]]
                m = slice(t * P, (t + 1) * P)
                for half in range(2):
                    split_mm(s[:, half], (lk_hi[:, h, m], lk_lo[:, h, m]), (lq_hi[:, halves(half)], lq_lo[:, halves(half)]),
                             True, False)
                    last = mm(s[:, half], sel[:, h], l_rows[:, half * (NB // 2):(half + 1) * (NB // 2)]
                              .rearrange("p a b -> p (a b)"), False, True)
                last.then_inc(st_pe, 1)

            def by_head(s, lhsT, ready):
                for half in range(2):
                    for t in range(MT):
                        for h in range(HEADS):
                            last = mm(slot[s][HD * h:HD * (h + 1), half], lhsT(t, h), probs[:, h * MT + t, halves(half)],
                                      t == 0, t == MT - 1)
                last.then_inc(ready, 1)

            def step(b, first, last):
                conv = NoConvolution() if first else Convolution(b - 1)
                if first:
                    pe.wait_ge(c_in, CONST_LOADS)
                    group_means(b, 0)
                    pe.wait_ge(w_ready, 5)
                    pe.wait_ge(gn_c[0], N_GN)
                pe.wait_ge(xhi_ready, (b + 1) * KT)
                pe.wait_ge(xlo_ready, (b + 1) * KT)
                project(0, WQ)
                wait_count(pe, y_ready, b * KT)
                project(1, WK)
                if not first:
                    group_means(b - 1, 1)
                    pe.wait_ge(gn_c[1], (b - 1) * N_GN + GN_SENT + 1)
                project(2, WV)
                pe.wait_ge(qkv_sb, b * 3 + 1)
                project(0, WLQ)
                pe.wait_ge(qkv_sb, b * 3 + 2)
                pe.wait_ge(pool_c, (b + 1) * N_POOL)
                for k in range(KT):
                    split_mm(slot[1][:, 0, 0:G], (w_hi[:, k, WLK:WLK + P], w_lo[:, k, WLK:WLK + P]),
                             (pool_hi[:, k], pool_lo[:, k]), k == 0, k == KT - 1)
                for t in range(MT):
                    m = slice(t * P, (t + 1) * P)
                    for k in range(KT):
                        ins = split_mm(slot[1][:, 1, m], (pool_hi[:, k, m], pool_lo[:, k, m]),
                                       (w_hi[:, k, WLV:WLV + P], w_lo[:, k, WLV:WLV + P]), k == 0, k == KT - 1)
                ins.then_inc(proj_pe, 1)
                for n in range(NB):
                    if n == 0:
                        pe.wait_ge(lk_act, b * 5 + HEADS)
                        pe.wait_ge(lq_dve, b + 1)
                    elif n == 1:
                        pe.wait_ge(lk_act, (b + 1) * 5)
                        pe.wait_ge(lk_dve, (b + 1) * HEADS)
                    elif n == 2:
                        pe.wait_ge(qkv_sb, b * 3 + 3)
                    else:
                        pe.wait_ge(la_max, b * NB + n - 2)
                    for half in range(2):
                        ins = mm(slot[LA_SLOT[n]][:, half], lq_hi[:, n * P:(n + 1) * P],
                                 lk_hi[:, half * 2:half * 2 + 2].rearrange("p a b -> p (a b)"), True, True)
                    ins.then_inc(la_pe, 1)
                    if n >= 2:
                        conv.more(7)
                pe.wait_ge(la_max, (b + 1) * NB)
                if first:
                    pe.wait_ge(zeroed_dve, 1)
                nc.tensor.transpose(slot[2][:, 0, 0:P], l_max[:], cst[:, C_ID:C_ID + P]).then_inc(lmt_pe, 1)
                conv.more(6)
                for j in range(NW):
                    pe.wait_ge(prod_ready, b * NW + j + 1)
                    for half in range(2):
                        ins = mm(slot[0][HD * j:HD * (j + 1), half], cst[:, C_HEAD:C_HEAD + HD], qk[:, j, halves(half)],
                                 True, True)
                ins.then_inc(ssum_pe, 1)
                conv.more(8)
                pe.wait_ge(ssum_sb, b + 1)
                pe.wait_ge(lrows, b + 1)
                for n in range(NB):
                    ins = nc.tensor.transpose(slot[2][:, n // 4, (n % 4) * P:(n % 4 + 1) * P],
                                              q_w[:, n * P:(n + 1) * P], cst[:, C_ID:C_ID + P])
                ins.then_inc(stok_pe, 1)
                conv.more(16)
                for i in range(LT - NW):
                    if i >= 2:
                        pe.wait_ge(st_exp, b * LT + i - 1)
                    pooled_scores(b, i)
                    conv.more(2)
                pe.wait_ge(soft_c, (b + 1) * N_SOFT)
                for n in range(NB):
                    ins = nc.tensor.transpose(slot[2][:, n // 4, (n % 4) * P:(n % 4 + 1) * P],
                                              s_soft[:, n].rearrange("p j h -> p (j h)"), cst[:, C_ID:C_ID + P])
                ins.then_inc(pt_pe, 1)
                conv.more(10)
                pe.wait_ge(pt_act, b + 1)
                pe.wait_ge(pt_dve, b + 1)
                for j in range(NW):
                    if j < 2:
                        pe.wait_ge(st_exp, b * LT + j + 3)
                    elif j == 3:
                        pe.wait_ge(pv_ready, b * NW + 1)
                    for half in range(2):
                        for part, p in enumerate((p_hi, p_lo)):
                            ins = mm(slot[PB_SLOT[j]][:, half], sel[:, HEADS + j], p[:, halves(half)], part == 0, part == 1)
                    ins.then_inc(pb_pe, 1)
                    conv.more(3)
                pe.wait_ge(pv_ready, b * NW + 2)
                if not last:
                    group_means(b + 1, 0)
                for i in range(LT - NW, LT):
                    if i == 4 and not last:
                        pe.wait_ge(gn_c[0], (b + 1) * N_GN + GN_SENT + 1)
                    elif i in (5, 6):
                        pe.wait_ge(pv_ready, b * NW + i - 2)
                    elif i == 7:
                        pe.wait_ge(st_exp, b * LT + 5)
                    pooled_scores(b, i)
                    conv.more(6)
                pe.wait_ge(st_exp, (b + 1) * LT)
                by_head(2, lambda t, h: cst[:, C_ONE:C_ONE + HD], lden_pe)
                by_head(0, lambda t, h: lv[:, t, HD * h:HD * (h + 1)], lpv_pe)
                pe.wait_ge(pv_dve, b + 1)
                for half in range(2):
                    ins = mm(slot[1][:, half], w_out[:, 0], q_w[:, halves(half)], True, True)
                ins.then_inc(out_pe, 1)
                conv.more(40)
                pe.wait_ge(lnorm, b + 1)
                for half in range(2):
                    ins = mm(slot[2][:, half], w_out[:, 1], k_w[:, halves(half)], True, True)
                ins.then_inc(out_pe, 1)
                conv.more(GROUPS * CONV_MM)

            pe.wait_ge(zeroed, 4)
            run_conv_weights = cw_split
            step(0, True, False)
            pe.wait_ge(run_conv_weights, 2)
            with pe.Fori(1, B - 1) as b:
                step(b, False, False)
            step(B - 1, False, True)
            group_means(B - 1, 1)
            Convolution(B - 1).more(GROUPS * CONV_MM)


def constants():
    import numpy as np
    c, s = np.zeros((P, C_ALL), np.float32), np.zeros((P, SEL_COLS), np.float32)
    p = np.arange(P)
    c[:, C_ID:C_ID + P] = np.eye(P)
    c[:, C_GRP:C_GRP + P] = (p[:, None] // GROUP == p[None] // GROUP) / GROUP
    for h in range(HEADS):
        c[:, C_HEAD + h] = p // HD == h
        s[:, h * P:(h + 1) * P] = ((p % HEADS == h) & (p < NB * HEADS))[:, None]
    c[:, C_ONE:C_ONE + HD] = 1
    for j in range(NW):
        s[:, (HEADS + j) * P:(HEADS + j + 1) * P] = p[:, None] == HD * j + p[None] // HD
    for n in range(NB):
        c[:, C_BLK + n] = p // HEADS == n
    c[:, C_IX:C_IX + H] = np.arange(1, H + 1)
    c[:, C_POS:C_POS + H] = np.linspace(-1, 1, H)
    return c, s


def kernel(x, L0_conv_h_qkv_w, L0_conv_h_proj_w, L0_conv_h_proj_b, L0_conv_l_q_w, L0_conv_l_kv_w, L0_conv_l_proj_w,
           L0_conv_l_proj_b, L1_conv_weight, L1_conv_bias, L1_conv_mask_weight, L1_conv_filter):
    import numpy as np
    import concourse.bacc as bacc
    from concourse.bass_utils import run_bass_kernel_spmd

    tiles = lambda a: np.ascontiguousarray(np.asarray(a).reshape(KT, P, -1))
    cols = lambda a: np.ascontiguousarray(np.asarray(a).reshape(-1, P).T)
    arrays = {
        "x": np.ascontiguousarray(np.asarray(x).reshape(B, KT, P, HW)),
        "h_qkv": tiles(L0_conv_h_qkv_w), "l_q": tiles(L0_conv_l_q_w), "l_kv": tiles(L0_conv_l_kv_w),
        "h_proj": np.ascontiguousarray(L0_conv_h_proj_w), "l_proj": np.ascontiguousarray(L0_conv_l_proj_w),
        "h_bias": cols(L0_conv_h_proj_b), "l_bias": cols(L0_conv_l_proj_b),
        "conv_w": tiles(np.asarray(L1_conv_weight).reshape(C, C, TAPS).transpose(1, 2, 0)),
        "conv_b": cols(L1_conv_bias), "mask_w": cols(L1_conv_mask_weight), "filt": cols(L1_conv_filter),
        "consts": constants()[0], "selectors": constants()[1],
    }
    nc = bacc.Bacc("TRN2", target_bir_lowering=False, num_devices=1)
    t = {n: nc.dram_tensor(n, a.shape, F32, kind="ExternalInput").ap() for n, a in arrays.items()}
    out = nc.dram_tensor("out", (B, KT, P, HW), F32, kind="ExternalOutput").ap()
    build(nc, t["x"], (t["h_qkv"], t["l_q"], t["l_kv"]), t["h_proj"], t["l_proj"], t["h_bias"], t["l_bias"],
          t["conv_w"], t["conv_b"], t["mask_w"], t["filt"], t["consts"], t["selectors"], out)
    r = run_bass_kernel_spmd(nc, [arrays], core_ids=[0])
    return np.asarray(r.results[0]["out"]).reshape(B, C, H, W)
```

```python
from contextlib import ExitStack

import concourse.bass as bass
from concourse import mybir

F32 = mybir.dt.float32
F32R = mybir.dt.float32r
I32 = mybir.dt.int32
ALU = mybir.AluOpType
ACT = mybir.ActivationFunctionType
AX_X = mybir.AxisListType.X

P = 128
B, C, H, W = 4, 256, 32, 32
KT = C // P
HW = H * W
WS = 2
NW = WS * WS
HG, WG = H // WS, W // WS
G = HG * WG
HALF = 512
HEADS, HD = 4, 32
SCALE = HD ** -0.5
MT = G // P
LT = HEADS * MT
SC = 3 * HD
SM = SC + 2
NB = HW // P
TAPS = 9
PADW = W + 2
GROUP = 8
EPS = 1e-5
ROUND = 12582912.0
MAGIC = 0x5F3759DF
IX_SUM = float(W * H * (H + 1) // 2)
LIN = 2.0 / (H - 1)

C_ID, C_GRP, C_HEAD, C_ONE = 0, P, 2 * P, 2 * P + HD
C_IX = C_ONE + HD
C_POS = C_IX + H
C_ALL = C_POS + H
SEL_COLS = NW * P

WQ, WK, WV, WLQ, WLK, WLV = (P * i for i in range(6))
WCOLS = 6 * P

LA_SLOT = (0, 1, 2, 0, 1, 2, 0, 1)
ST_SLOT = (0, 1, 0, 1, 1, 2, 0, 1)
PB_SLOT = (0, 1, 2, 0)

GROUPS = 2 * KT
CONV_MM = KT * TAPS * 3
PAIR = 2 * CONV_MM
FRONT = (0, 10, 0, 0, 15, 5, 30, 6, 6, 8, 4, 12, 12)
REST = (8, 3, 10, 4, 6, 8)

N_GN, N_MASK, N_SOFT, N_POOL = 20, 17, 7, 4
GN_SENT, SOFT_READ = 4, 2


def wait_count(eng, sem, n):
    if not (isinstance(n, int) and n <= 0):
        eng.wait_ge(sem, n)


class Chain:

    def __init__(self, eng, sem, length, image):
        self.eng, self.sem, self.base, self.length, self.n = eng, sem, image * length, length, 0

    def __call__(self, ins):
        self.n += 1
        ins.then_inc(self.sem, 1)
        if self.n < self.length:
            self.eng.wait_ge(self.sem, self.base + self.n)


def build(nc, x, wqkv, whp, wlp, bh, bl, cw, cb, mw, filt, consts, selectors, out):
    with ExitStack() as ctx:
        def sb(name, shape, dt=F32):
            return ctx.enter_context(nc.sbuf_tensor(name, shape, dt))

        def sem(name):
            return ctx.enter_context(nc.semaphore(name))

        xy = sb("xy", [P, B * KT * HW])
        cst = sb("cst", [P, C_ALL])
        sel = sb("sel", [P, NW, P], F32R)
        w_hi = sb("w_hi", [P, KT, WCOLS], F32R)
        w_lo = sb("w_lo", [P, KT, WCOLS], F32R)
        w_out = sb("w_out", [P, 2, P])
        bias = sb("bias", [P, 2])
        cw_hi = sb("cw_hi", [P, KT * TAPS * C], F32R)
        cw_lo = sb("cw_lo", [P, KT * TAPS * C], F32R)
        cbias = sb("cbias", [P, KT])
        mwf = sb("mwf", [P, 3, KT])
        xn = sb("xn", [P, KT, HW])
        xn_hi = sb("xn_hi", [P, KT, HW], F32R)
        xn_lo = sb("xn_lo", [P, KT, HW], F32R)
        p_w = xn_lo[:, 0]
        pool_hi = sb("pool_hi", [P, KT, G], F32R)
        pool_lo = sb("pool_lo", [P, KT, G], F32R)
        q_w = sb("q_w", [P, HW])
        k_w = sb("k_w", [P, HW])
        v_w = sb("v_w", [P, HW])
        qs = sb("qs", [P, HEADS, HW], F32R)
        ks = sb("ks", [P, HEADS, G], F32R)
        lv = sb("lv", [P, MT, P])
        probs = sb("probs", [P, LT, HW])
        qk = probs[:, LT - NW:LT, :]
        lq_hi, lq_lo = probs[:, 0].bitcast(F32R), probs[:, 1]
        lk_hi, lk_lo = probs[:, 2, 0:G].bitcast(F32R), probs[:, 2, G:2 * G]
        lm_hi, lm_lo = probs[0:NB * HEADS, 3, 0:P].bitcast(F32R), probs[0:NB * HEADS, 3, P:2 * P]
        raw = qk.rearrange("p a b -> p (a b)")
        raw_w = raw[:, 0:KT * WCOLS].rearrange("p (k n) -> p k n", k=KT)
        raw_sel = raw[:, KT * WCOLS:KT * WCOLS + SEL_COLS]
        s_soft = k_w[:].rearrange("p (n j r) -> p n j r", n=NB, j=NW)
        s_exp, s_hi = s_soft[:, :, :, 0:HEADS], s_soft[:, :, :, HEADS:2 * HEADS]
        s_max = sb("s_max", [P, NB, HEADS])
        s_den = sb("s_den", [P, NB, HEADS])
        l_max = sb("l_max", [P, P])
        im_hi = sb("im_hi", [P, KT, PADW * PADW], F32R)
        im_lo = sb("im_lo", [P, KT, PADW * PADW], F32R)
        mask = sb("mask", [P, KT, HW])
        pool_t, pool_s = mask[:, :, 0:2 * G], mask[:, :, 2 * G:3 * G]
        first_taps = (TAPS - 1) * C
        raw_cw = [((0, first_taps), xy[:, (B - KT + k) * KT * HW:][:, 0:first_taps]) for k in range(KT)]
        raw_cw = [(raw_cw[k], ((first_taps, TAPS * C), mask[:, k, 3 * G:])) for k in range(KT)]
        st = [sb(f"st{i}", [P, KT, 2, 6]) for i in range(2)]
        mv = [sb(f"mv{i}", [P, KT, 2]) for i in range(2)]
        gn = [sb(f"gn{i}", [P, 8, KT]) for i in range(2)]
        rc = sb("rc", [P, KT, 2, H])
        rw = sb("rw", [P, KT, 2, H])
        mu = sb("mu", [P, KT, 2])
        idle = sb("idle", [P, 1])
        sx = gn[1][:, 2:4]

        cps = ctx.enter_context(nc.psum_tensor("cps", [P, 2, HALF], F32))
        slot = [ctx.enter_context(nc.psum_tensor(f"slot{i}", [P, 2, HALF], F32)) for i in range(3)]
        flat = [s[:].rearrange("p a b -> p (a b)") for s in slot]

        x_in = [sem(f"x_in{b}") for b in range(B)]
        w_in, cw_in, c_in, cst_in = sem("w_in"), sem("cw_in"), sem("c_in"), sem("cst_in")
        w_split = sem("w_split")
        out_done = sem("out_done")
        w_ready = sem("w_ready")
        cw_split = sem("cw_split")
        zeroed = sem("zeroed")
        im_free = sem("im_free")
        zeroed_dve = sem("zeroed_dve")
        gn_c = [sem("gn1_c"), sem("gn2_c")]
        gn_pe = [sem("gn1_pe"), sem("gn2_pe")]
        mask_c, soft_c, pool_c = sem("mask_c"), sem("soft_c"), sem("pool_c")
        xhi_ready, xn_ready = sem("xhi_ready"), sem("xn_ready")
        xlo_ready = sem("xlo_ready")
        proj_pe = sem("proj_pe")
        qkv_sb = sem("qkv_sb")
        lq_act, lq_dve = sem("lq_act"), sem("lq_dve")
        lk_act, lk_dve = sem("lk_act"), sem("lk_dve")
        stacked, max_stacked = sem("stacked"), sem("max_stacked")
        prod_ready = sem("prod_ready")
        ssum_pe, ssum_sb = sem("ssum_pe"), sem("ssum_sb")
        stok_pe, sexp = sem("stok_pe"), sem("sexp")
        pt_pe, pt_act = sem("pt_pe"), sem("pt_act")
        la_pe, la_max = sem("la_pe"), sem("la_max")
        lmt_pe, lm_dve = sem("lmt_pe"), sem("lm_dve")
        pb_pe, pv_ready = sem("pb_pe"), sem("pv_ready")
        pv_pool, pv_dve = sem("pv_pool"), sem("pv_dve")
        st_pe, st_exp = sem("st_pe"), sem("st_exp")
        lden_pe, linv = sem("lden_pe"), sem("linv")
        lpv_pe, lnorm = sem("lpv_pe"), sem("lnorm")
        out_pe, y_ready = sem("out_pe"), sem("y_ready")
        yn_ready = sem("yn_ready")
        msum, masked = sem("msum"), sem("masked")
        im_act, im_dve = sem("im_act"), sem("im_dve")
        conv_pe, conv_out = sem("conv_pe"), sem("conv_out")

        block = ctx.enter_context(nc.Block())

        def img(b, k, lo=0, n=HW):
            return xy[:, bass.ds(b * (KT * HW) + (k * HW + lo), n)]

        def run(eng, step):
            step(0, True, False)
            with eng.Fori(1, B - 1) as b:
                step(b, False, False)
            step(B - 1, False, True)

        @block.sync
        def _(sp):
            def load(b):
                for k in range(KT):
                    sp.dma_start(img(b, k), x[b, k]).then_inc(x_in[b], 16)

            sp.dma_start(cst[:], consts).then_inc(cst_in, 16)
            for b in range(B - KT):
                load(b)
                if b == 0:
                    for c0, src in zip((WQ, WLQ, WLK), wqkv):
                        for k in range(KT):
                            sp.dma_start(raw_w[:, k, c0:c0 + src.shape[2]], src[k]).then_inc(w_in, 16)
                    for dst, src in ((raw_sel, selectors), (w_out[:, 0], whp), (w_out[:, 1], wlp), (bias[:, 0:1], bh), (bias[:, 1:2], bl),
                                     (cbias[:], cb), (mwf[:, 0], mw), (mwf[:, 1], filt)):
                        sp.dma_start(dst, src).then_inc(c_in, 16)
                    for k in range(KT):
                        for (c0, c1), to in raw_cw[k]:
                            sp.dma_start(to, cw[k][:, c0:c1]).then_inc(cw_in, 16)

            def store(b, o, count):
                sp.wait_ge(conv_out, count)
                sp.dma_start(out[bass.ds(b, 1), o].rearrange("b p n -> p (b n)"), img(b, o)).then_inc(out_done, 16)

            def stack(count, count_k):
                def rows(to, part, parts):
                    sp.dma_start(to[HD * part:HD * (part + 1)].bitcast(F32), parts.bitcast(F32)).then_inc(stacked, 16)

                sp.wait_ge(lq_act, count)
                rows(qs, 0, lq_hi)
                rows(qs, 2, lq_hi)
                sp.wait_ge(lq_dve, count)
                rows(qs, 1, lq_lo)
                sp.wait_ge(lk_act, count_k)
                rows(ks, 0, lk_hi)
                rows(ks, 1, lk_hi)
                sp.wait_ge(lk_dve, count)
                rows(ks, 2, lk_lo)

            def stack_maxima(count):
                sp.wait_ge(lm_dve, count)
                for i, t in enumerate((lm_hi, lm_lo)):
                    sp.dma_start(qs[SC + i:SC + i + 1].bitcast(F32), t.bitcast(F32)).then_inc(max_stacked, 16)

            def step(b, first, last):
                counts = (b - 1, (b + 1) * GROUPS - 2, (b + 1) * GROUPS, b + 2, b * 2 + 3, b * 2 + 4)
                if not (first or last):
                    counts = [sp.snap(n) for n in counts]
                prev, tile_0, tile_1, parts, parts_k, parts_max = counts
                if first:
                    for k in range(KT):
                        sp.wait_ge(cw_split, 2 * KT + 2 * (k + 1))
                        load(B - KT + k)
                else:
                    store(prev, 0, tile_0)
                if not last:
                    stack(parts, parts_k)
                    stack_maxima(parts_max)
                if not first:
                    store(prev, 1, tile_1)

            stack(1, 1)
            stack_maxima(2)
            run(sp, step)
            for o in range(KT):
                store(B - 1, o, B * GROUPS + 2 * (o + 1))
            sp.wait_ge(out_done, B * KT * 16)

        CONST_LOADS = 8 * 16
        STACK, MAX_STACK = 6 * 16, 2 * 16

        @block.gpsimd
        def _(pool):
            def mask_sum(b, pooled):
                pool.wait_ge(mask_c, (b + 1) * N_MASK)
                pool.wait_ge(pool_c, pooled * N_POOL)
                for k in range(KT):
                    nc.gpsimd.tensor_tensor(mask[:, k].rearrange("p (h w) -> p h w", h=H),
                                            rw[:, k, 0].unsqueeze(2).to_broadcast([P, H, W]),
                                            rw[:, k, 1].unsqueeze(1).to_broadcast([P, H, W]),
                                            ALU.add).then_inc(msum, 1)

            def products(b, keys):
                for j in keys:
                    nc.gpsimd.tensor_tensor(
                        qk[:, j].rearrange("p (n w) -> p n w", n=NW),
                        q_w[:].rearrange("p (n w) -> p n w", n=NW),
                        k_w[:, j * G:(j + 1) * G].unsqueeze(1).to_broadcast([P, NW, G]),
                        ALU.mult).then_inc(prod_ready, 1)

            def split_conv_weights():
                pool.wait_ge(cw_in, 2 * KT * 16)
                pieces = [(k * TAPS * C, cols, src) for k in range(KT) for cols, src in raw_cw[k]]
                for base, (c0, c1), src in pieces:
                    nc.gpsimd.tensor_scalar(cw_hi[:, base + c0:base + c1], src, 1.0, 0.0, ALU.mult,
                                            ALU.add).then_inc(cw_split, 1)
                for i, (base, (c0, c1), src) in enumerate(pieces):
                    pool.wait_ge(cw_split, 2 * KT + i)
                    nc.gpsimd.tensor_tensor(cw_lo[:, base + c0:base + c1], src, cw_hi[:, base + c0:base + c1].bitcast(F32),
                                            ALU.subtract).then_inc(cw_split, 1)

            def step(b, first, last):
                pool.wait_ge(qkv_sb, b * 3 + 2)
                wait_count(pool, lpv_pe, b)
                products(b, range(NW))
                if first:
                    split_conv_weights()
                else:
                    mask_sum(b - 1, b + 1)
                pool.wait_ge(pv_ready, b * NW + 2)
                nc.gpsimd.tensor_tensor(qk[:, 0], qk[:, 0], qk[:, 1], ALU.add).then_inc(pv_pool, 1)

            nc.gpsimd.memset(im_hi[:].bitcast(F32), 0.0).then_inc(zeroed, 1)
            pool.wait_ge(zeroed, 1)
            nc.gpsimd.memset(im_lo[:].bitcast(F32), 0.0).then_inc(im_free, 1)
            pool.wait_ge(w_split, 1)
            nc.gpsimd.tensor_tensor(w_lo[:], raw_w, w_hi[:].bitcast(F32), ALU.subtract).then_inc(w_split, 1)
            pool.wait_ge(w_split, 2)
            pool.wait_ge(w_ready, 3)
            run(pool, step)
            mask_sum(B - 1, B)

        @block.scalar
        def _(act):
            def normalise(b, first=False):
                act.wait_ge(gn_c[0], (b + 1) * N_GN)
                wait_count(act, xlo_ready, b * KT)
                wait_count(act, pool_c, b * N_POOL)
                for k in range(KT):
                    src = img(b, k).rearrange("p (hg a wg b) -> p a b hg wg", hg=HG, a=WS, wg=WG, b=WS)
                    for t, ready in ((xn_hi, xhi_ready), (xn, xn_ready))[0:1 if first else 2]:
                        dst = t[:, k].rearrange("p (a b hg wg) -> p a b hg wg", a=WS, b=WS, hg=HG)
                        for a in range(WS):
                            last = nc.scalar.activation(dst[:, a], src[:, a], ACT.Identity,
                                                        bias=gn[0][:, 6, k:k + 1], scale=gn[0][:, 5, k:k + 1])
                        last.then_inc(ready, 1)

            def projections(b):
                wait_count(act, lpv_pe, b)
                act.wait_ge(proj_pe, b * 5 + 1)
                nc.scalar.copy(lq_hi, flat[0]).then_inc(lq_act, 1)
                act.wait_ge(proj_pe, b * 5 + 2)
                nc.scalar.copy(lk_hi, slot[1][:, 0, 0:G]).then_inc(lk_act, 1)
                nc.scalar.activation(lv[:].rearrange("p a b -> p (a b)"), slot[1][:, 1, 0:MT * P], ACT.Copy,
                                     scale=1.0 / NW).then_inc(lk_act, 1)
                wait_count(act, y_ready, b * KT)
                for i, (s, dst) in enumerate(((2, q_w), (0, k_w), (1, v_w))):
                    act.wait_ge(proj_pe, b * 5 + i + 3)
                    nc.scalar.copy(dst[:], flat[s]).then_inc(qkv_sb, 1)

            def normalise_y(b, normalised):
                act.wait_ge(gn_c[1], (b + 1) * N_GN)
                act.wait_ge(xlo_ready, normalised * KT)
                act.wait_ge(pool_c, normalised * N_POOL)
                for k in range(KT):
                    nc.scalar.activation(xn[:, k], img(b, k), ACT.Identity, bias=gn[1][:, 6, k:k + 1],
                                         scale=gn[1][:, 5, k:k + 1]).then_inc(yn_ready, 1)

            def conv_input(b, k):
                act.wait_ge(masked, b * KT + k + 1)
                inner = im_hi[:, k].rearrange("p (h w) -> p h w", h=PADW)[:, 1:H + 1, 1:W + 1]
                nc.scalar.activation(inner, mask[:, k].rearrange("p (h w) -> p h w", h=H), ACT.Relu).then_inc(im_act, 1)

            def exp_scores(b, tiles):
                for i in tiles:
                    act.wait_ge(st_pe, b * LT + i + 1)
                    nc.scalar.activation(probs[:, i], flat[ST_SLOT[i]], ACT.Exp, scale=SCALE / NW)\
                        .then_inc(st_exp, 1)

            def step(b, first, last):
                if first:
                    act.wait_ge(w_in, 3 * KT * 16)
                    nc.scalar.copy(w_hi[:], raw_w).then_inc(w_split, 1)
                    normalise(b, first=True)
                projections(b)
                if not first:
                    normalise_y(b - 1, b + 1)
                    conv_input(b - 1, 0)
                act.wait_ge(ssum_pe, b + 1)
                scores = cps[:].rearrange("p a b -> p (a b)") if first else flat[0]
                nc.scalar.copy(q_w[:], scores).then_inc(ssum_sb, 1)
                act.wait_ge(soft_c, b * N_SOFT + SOFT_READ)
                nc.scalar.activation(s_exp, s_exp, ACT.Exp, scale=SCALE).then_inc(sexp, 1)
                exp_scores(b, range(2))
                if not first:
                    conv_input(b - 1, 1)
                exp_scores(b, range(2, LT - NW))
                act.wait_ge(pt_pe, b + 1)
                nc.scalar.copy(p_w, flat[2]).then_inc(pt_act, 1)
                act.wait_ge(pv_dve, (b + 1) * 2)
                exp_scores(b, range(LT - NW, LT))
                if not last:
                    normalise(b + 1)

            run(act, step)
            normalise_y(B - 1, B)
            for k in range(KT):
                conv_input(B - 1, k)

        @block.vector
        def _(dve):
            def statistics(b, i, meanwhile=None):
                link = Chain(dve, gn_c[i], N_GN, b)
                s, m, g = st[i], mv[i], gn[i]
                for k in range(KT):
                    for half in range(2):
                        last = nc.vector.bn_stats(s[:, k, half], img(b, k, half * HALF, HALF))
                link(last)
                nc.vector.memset(g[:, 7], 0.0)
                for k in range(KT):
                    last = nc.vector.bn_aggr(m[:, k], s[:, k].rearrange("p a b -> p (a b)"))
                link(last)
                link(nc.vector.tensor_tensor(g[:, 2], m[:, :, 0], m[:, :, 0], ALU.mult))
                link(nc.vector.tensor_tensor(m[:, :, 1], m[:, :, 1], g[:, 2], ALU.add))
                if meanwhile:
                    meanwhile()
                dve.wait_ge(gn_pe[i], b + 1)
                src = slot[2][:, 0, 0:2 * KT].rearrange("p (k s) -> p s k", s=2)
                link(nc.vector.tensor_copy(g[:, 0:2], src))
                link(nc.vector.tensor_tensor(g[:, 2], g[:, 0], g[:, 0], ALU.mult))
                link(nc.vector.scalar_tensor_tensor(g[:, 3], g[:, 1], EPS, g[:, 2], ALU.add, ALU.subtract))
                link(nc.vector.tensor_scalar(g[:, 4], g[:, 3], -0.5, None, ALU.mult))
                link(nc.vector.tensor_scalar(g[:, 7].bitcast(I32), g[:, 3].bitcast(I32), 1, None,
                                             ALU.logical_shift_right))
                link(nc.vector.tensor_scalar(g[:, 5].bitcast(I32), g[:, 7].bitcast(I32), -1.0, float(MAGIC),
                                             ALU.mult, ALU.add))
                for _ in range(3):
                    link(nc.vector.tensor_tensor(g[:, 7], g[:, 5], g[:, 5], ALU.mult))
                    link(nc.vector.tensor_tensor(g[:, 7], g[:, 7], g[:, 4], ALU.mult))
                    link(nc.vector.scalar_tensor_tensor(g[:, 5], g[:, 7], 1.5, g[:, 5], ALU.add, ALU.mult))
                link(nc.vector.scalar_tensor_tensor(g[:, 6], g[:, 0], -1.0, g[:, 5], ALU.mult, ALU.mult))
                assert link.n == N_GN

            def split_input(b):
                wait_count(dve, proj_pe, b * 5)
                for k in range(KT):
                    dve.wait_ge(xhi_ready, b * KT + k + 1)
                    dve.wait_ge(xn_ready, b * KT + k + 1)
                    nc.vector.tensor_tensor(xn_lo[:, k], xn[:, k], xn_hi[:, k].bitcast(F32),
                                            ALU.subtract).then_inc(xlo_ready, 1)

            def pooling(b):
                link = Chain(dve, pool_c, N_POOL, b)
                link(nc.vector.tensor_tensor(pool_t, xn[:, :, 0:2 * G], xn[:, :, 2 * G:4 * G], ALU.add))
                link(nc.vector.tensor_tensor(pool_s, pool_t[:, :, 0:G], pool_t[:, :, G:2 * G], ALU.add))
                link(nc.vector.tensor_copy(pool_hi[:], pool_s))
                link(nc.vector.tensor_tensor(pool_lo[:], pool_s, pool_hi[:].bitcast(F32), ALU.subtract))

            def line_sums(b):
                carry()
                y = xy[:, bass.ds(b * (KT * HW), KT * HW)]
                nc.vector.tensor_reduce(rc[:, :, 0], y.rearrange("p (k h w) -> p k h w", k=KT, h=H), AX_X, ALU.add)
                nc.vector.tensor_reduce(rc[:, :, 1], y.rearrange("p (k h w) -> p k w h", k=KT, h=H), AX_X,
                                        ALU.add).then_inc(mask_c, 1)

            def mask_parts(b):
                link = Chain(dve, mask_c, N_MASK, b)
                link.n = 1
                dve.wait_ge(mask_c, b * N_MASK + 1)
                g = gn[1]
                both = [t[:].rearrange("p k s n -> p (k s) n") for t in (rc, rw)]
                m4 = mu[:].rearrange("p k s -> p (k s)")
                link(nc.vector.tensor_tensor(both[1], both[0],
                                             cst[:, C_IX:C_IX + H].unsqueeze(1).to_broadcast([P, 2 * KT, H]), ALU.mult))
                link(nc.vector.tensor_reduce(m4, both[1], AX_X, ALU.add))
                link(nc.vector.tensor_tensor(sx[:, 0], mv[1][:, :, 0], g[:, 0], ALU.subtract))
                link(nc.vector.scalar_tensor_tensor(sx[:, 0], sx[:, 0], float(HW), g[:, 5], ALU.mult, ALU.mult))
                link(nc.vector.tensor_scalar(sx[:, 0], sx[:, 0], 1e-9, None, ALU.max))
                link(nc.vector.reciprocal(sx[:, 1], sx[:, 0]))
                link(nc.vector.tensor_tensor(sx[:, 1], sx[:, 1], g[:, 5], ALU.mult))
                link(nc.vector.scalar_tensor_tensor(mu[:], g[:, 0].unsqueeze(2).to_broadcast([P, KT, 2]), -IX_SUM,
                                                    mu[:], ALU.mult, ALU.add))
                link(nc.vector.tensor_tensor(mu[:], mu[:], sx[:, 1].unsqueeze(2).to_broadcast([P, KT, 2]), ALU.mult))
                link(nc.vector.tensor_scalar(m4, m4, 1.0, float(H), ALU.max, ALU.min))
                link(nc.vector.tensor_scalar(m4, m4, ROUND, -ROUND, ALU.add, ALU.add))
                link(nc.vector.tensor_scalar(m4, m4, LIN, -1.0 - LIN, ALU.mult, ALU.add))
                link(nc.vector.tensor_tensor(both[0], cst[:, C_POS:C_POS + H].unsqueeze(1).to_broadcast([P, 2 * KT, H]),
                                             m4.unsqueeze(2).to_broadcast([P, 2 * KT, H]), ALU.subtract))
                link(nc.vector.scalar_tensor_tensor(both[1], both[0], -1.0, both[0], ALU.mult, ALU.max))
                link(nc.vector.tensor_tensor(rw[:].rearrange("p k s n -> p k (s n)"),
                                             rw[:].rearrange("p k s n -> p k (s n)"),
                                             mwf[:, 2].unsqueeze(2).to_broadcast([P, KT, 2 * H]), ALU.mult))
                link(nc.vector.tensor_scalar(rw[:, :, 0], rw[:, :, 0], 1.0, None, ALU.add))
                assert link.n == N_MASK

            def masked_image(b, k):
                if k == 0:
                    dve.wait_ge(im_free, b + 1)
                dve.wait_ge(msum, b * KT + k + 1)
                dve.wait_ge(yn_ready, b * KT + k + 1)
                nc.vector.scalar_tensor_tensor(mask[:, k], mask[:, k], -1.0, xn[:, k], ALU.max,
                                               ALU.mult).then_inc(masked, 1)

            def image_lo(b, k):
                dve.wait_ge(im_act, b * KT + k + 1)
                inner = [t[:, k].rearrange("p (h w) -> p h w", h=PADW)[:, 1:H + 1, 1:W + 1] for t in (im_hi, im_lo)]
                nc.vector.scalar_tensor_tensor(inner[1], mask[:, k].rearrange("p (h w) -> p h w", h=H), 0.0,
                                               inner[0].bitcast(F32), ALU.max, ALU.subtract).then_inc(im_dve, 1)

            def pooled_lo(b):
                dve.wait_ge(lq_act, b + 1)
                nc.vector.tensor_tensor(lq_lo, flat[0], lq_hi.bitcast(F32), ALU.subtract).then_inc(lq_dve, 1)
                dve.wait_ge(lk_act, b * 2 + 2)
                nc.vector.tensor_tensor(lk_lo, slot[1][:, 0, 0:G], lk_hi.bitcast(F32), ALU.subtract).then_inc(lk_dve, 1)

            def maxima(b, blocks):
                for n in blocks:
                    dve.wait_ge(la_pe, b * NB + n + 1)
                    nc.vector.tensor_reduce(l_max[:, bass.ds(n, HEADS, step=NB)],
                                            flat[LA_SLOT[n]].rearrange("p (h m) -> p h m", h=HEADS), AX_X, ALU.max,
                                            negate=True).then_inc(la_max, 1)

            def maxima_parts(b):
                dve.wait_ge(lmt_pe, b + 1)
                rows = slot[2][0:NB * HEADS, 0, 0:P]
                nc.vector.tensor_copy(lm_hi, rows).then_inc(lm_dve, 1)
                dve.wait_ge(lm_dve, b * 2 + 1)
                nc.vector.tensor_tensor(lm_lo, rows, lm_hi.bitcast(F32), ALU.subtract).then_inc(lm_dve, 1)

            def window_softmax(b):
                link = Chain(dve, soft_c, N_SOFT, b)
                dve.wait_ge(stok_pe, b + 1)
                s = flat[2].rearrange("p (n j h) -> p n j h", n=NB, j=NW)[:, :, :, 0:HEADS]
                e = s_exp
                link(nc.vector.tensor_reduce(s_max[:], s.rearrange("p n j h -> p n h j"), AX_X, ALU.max))
                link(nc.vector.tensor_tensor(e, s, s_max[:].unsqueeze(2).to_broadcast([P, NB, NW, HEADS]), ALU.subtract))
                dve.wait_ge(sexp, b + 1)
                link(nc.vector.tensor_reduce(s_den[:], e.rearrange("p n j h -> p n h j"), AX_X, ALU.add))
                link(nc.vector.reciprocal(s_max[:], s_den[:]))
                link(nc.vector.tensor_tensor(e, e, s_max[:].unsqueeze(2).to_broadcast([P, NB, NW, HEADS]), ALU.mult))
                link(nc.vector.tensor_copy(s_hi.bitcast(F32R), e))
                link(nc.vector.tensor_tensor(e, e, s_hi, ALU.subtract))

            def conv_result(b, groups):
                for g in groups:
                    o, half = divmod(g, 2)
                    dve.wait_ge(conv_pe, b * GROUPS + g + 1)
                    dst = img(b, o, half * HALF, HALF)
                    nc.vector.scalar_tensor_tensor(dst, cps[:, g % 2], cbias[:, o:o + 1], dst, ALU.add,
                                                   ALU.add).then_inc(conv_out, 1)

            def residual(b, k, s):
                dve.wait_ge(out_pe, b * 2 + k + 1)
                y = img(b, k).rearrange("p (hg a wg b) -> p a b hg wg", hg=HG, a=WS, wg=WG, b=WS)
                for n in range(NW):
                    dst = y[:, n // WS, n % WS]
                    last = nc.vector.scalar_tensor_tensor(
                        dst, flat[s][:, n * G:(n + 1) * G].rearrange("p (hg wg) -> p hg wg", hg=HG),
                        bias[:, k:k + 1], dst, ALU.add, ALU.add)
                last.then_inc(y_ready, 1)

            def carry():
                nc.vector.memset(idle[:], 0.0)

            def masks(b):
                dve.wait_ge(y_ready, (b + 1) * KT)
                carry()
                statistics(b, 1, lambda: line_sums(b))

            def front(b, older=None, first=False):
                pooled_lo(b)
                if not first:
                    masks(b - 1)
                maxima(b, range(3))
                if not first:
                    mask_parts(b - 1)
                maxima(b, range(3, NB))
                maxima_parts(b)
                if not first:
                    masked_image(b - 1, 0)
                    image_lo(b - 1, 0)
                window_softmax(b)
                if older is not None:
                    conv_result(older, (2, 3))
                if not first:
                    masked_image(b - 1, 1)
                    image_lo(b - 1, 1)

            def step(b, first, last):
                for j in range(NW):
                    dve.wait_ge(pb_pe, b * NW + j + 1)
                    nc.vector.tensor_tensor(
                        qk[:, j].rearrange("p (n w) -> p n w", n=NW),
                        flat[PB_SLOT[j]].rearrange("p (n w) -> p n w", n=NW),
                        v_w[:, j * G:(j + 1) * G].unsqueeze(1).to_broadcast([P, NW, G]),
                        ALU.mult).then_inc(pv_ready, 1)
                if first:
                    dve.wait_ge(x_in[1], KT * 16)
                dve.wait_ge(pv_ready, (b + 1) * NW)
                nc.vector.tensor_tensor(qk[:, 2], qk[:, 2], qk[:, 3], ALU.add).then_inc(pv_dve, 1)
                dve.wait_ge(pv_dve, b * 2 + 1)
                dve.wait_ge(pv_pool, b + 1)
                nc.vector.tensor_tensor(q_w[:], qk[:, 0], qk[:, 2], ALU.add).then_inc(pv_dve, 1)
                if not last:
                    statistics(b + 1, 0)
                for half in range(2):
                    h = slice(half * HALF, (half + 1) * HALF)
                    dve.wait_ge(lden_pe, b * 2 + half + 1)
                    nc.vector.reciprocal(v_w[:, h], flat[2][:, h]).then_inc(linv, 1)
                residual(b, 0, 1)
                dve.wait_ge(linv, (b + 1) * 2)
                dve.wait_ge(lpv_pe, b + 1)
                nc.vector.tensor_tensor(k_w[:], flat[0], v_w[:], ALU.mult).then_inc(lnorm, 1)
                if not last:
                    split_input(b + 1)
                residual(b, 1, 2)
                if not last:
                    pooling(b + 1)
                if not first:
                    conv_result(b - 1, (0, 1))
                if first:
                    for i in range(B - KT, B):
                        dve.wait_ge(x_in[i], KT * 16)
                if last:
                    masks(b)
                else:
                    front(b + 1, None if first else b - 1)

            dve.wait_ge(x_in[0], KT * 16)
            statistics(0, 0)
            dve.wait_ge(gn_c[0], N_GN)
            for k in range(KT):
                src = img(0, k).rearrange("p (hg a wg b) -> p a b hg wg", hg=HG, a=WS, wg=WG, b=WS)
                dst = xn[:, k].rearrange("p (a b hg wg) -> p a b hg wg", a=WS, b=WS, hg=HG)
                for a in range(WS):
                    ins = nc.vector.tensor_scalar(dst[:, a], src[:, a], gn[0][:, 5, k:k + 1], gn[0][:, 6, k:k + 1],
                                                  ALU.mult, ALU.add)
                ins.then_inc(xn_ready, 1)
            split_input(0)
            pooling(0)
            dve.wait_ge(c_in, CONST_LOADS)
            nc.vector.tensor_copy(sel[:].rearrange("p a b -> p (a b)"), raw_sel).then_inc(w_ready, 1)
            nc.vector.memset(l_max[:], 0.0).then_inc(zeroed_dve, 1)
            nc.vector.memset(idle[:], 0.0).then_inc(conv_out, GROUPS)
            nc.vector.memset(ks[SC:SM].bitcast(F32), 1.0).then_inc(zeroed_dve, 1)
            nc.vector.scalar_tensor_tensor(mwf[:, 2], mwf[:, 1], 1.0, mwf[:, 0], ALU.is_equal,
                                           ALU.mult).then_inc(w_ready, 1)
            dve.wait_ge(w_ready, 2)
            nc.vector.tensor_scalar(mwf[:, 2], mwf[:, 2], -1.0, None, ALU.mult).then_inc(w_ready, 1)
            dve.wait_ge(w_ready, 3)
            front(0, first=True)
            run(dve, step)
            mask_parts(B - 1)
            masked_image(B - 1, 0)
            image_lo(B - 1, 0)
            conv_result(B - 2, (2, 3))
            masked_image(B - 1, 1)
            image_lo(B - 1, 1)
            conv_result(B - 1, range(GROUPS))

        @block.tensor
        def _(pe):
            def mm(dst, lhsT, rhs, start, stop):
                return nc.tensor.matmul(dst, lhsT, rhs, start=start, stop=stop)

            def split_mm(dst, lhsT, rhs, start=True, stop=True):
                mm(dst, lhsT[0], rhs[0], start, False)
                mm(dst, lhsT[0], rhs[1], False, False)
                return mm(dst, lhsT[1], rhs[0], False, stop)

            def halves(i):
                return slice(i * HALF, (i + 1) * HALF)

            class Convolution:

                def __init__(self, b):
                    self.b, self.at = b, 0

                def more(self, n):
                    b = self.b
                    for i in range(self.at, min(self.at + n, GROUPS * CONV_MM)):
                        o, m = divmod(i, PAIR)
                        k, m = divmod(m, CONV_MM)
                        half, m = divmod(m, CONV_MM // KT)
                        tap, part = divmod(m, 3)
                        begin, end = m == 0 and k == 0, m == CONV_MM // KT - 1 and k == KT - 1
                        if m == 0 and half == 0 and o == 0:
                            pe.wait_ge(im_act, b * KT + k + 1)
                            pe.wait_ge(im_dve, b * KT + k + 1)
                        if begin:
                            pe.wait_ge(conv_out, (b + 1) * GROUPS + 2 * (o - 1) + half + 1)
                        dy, dx = divmod(tap, 3)
                        c0 = (k * TAPS + tap) * C + o * P
                        im = (im_hi, im_lo, im_hi)[part][:, k].rearrange("p (h w) -> p h w", h=PADW)
                        y0 = dy + half * (H // 2)
                        ins = mm(cps[:, half].rearrange("p (h w) -> p h w", w=W),
                                 (cw_hi, cw_hi, cw_lo)[part][:, c0:c0 + P],
                                 im[:, y0:y0 + H // 2, dx:dx + W], begin, end)
                        if end:
                            ins.then_inc(conv_pe, 1)
                        elif m == CONV_MM // KT - 1 and half == 1 and o == KT - 1:
                            ins.then_inc(im_free, 1)
                    self.at += n

            class NoConvolution:
                at = 0

                def more(self, n):
                    pass

            def group_means(b, i):
                pe.wait_ge(gn_c[i], b * N_GN + GN_SENT)
                mm(slot[2][:, 0, 0:2 * KT], cst[:, C_GRP:C_GRP + P], mv[i][:].rearrange("p k s -> p (k s)"),
                   True, True).then_inc(gn_pe[i], 1)

            def project(s, c0):
                for i in range(2):
                    for k in range(KT):
                        last = split_mm(slot[s][:, i], (w_hi[:, k, c0:c0 + P], w_lo[:, k, c0:c0 + P]),
                                        (xn_hi[:, k, halves(i)], xn_lo[:, k, halves(i)]), k == 0, k == KT - 1)
                last.then_inc(proj_pe, 1)

            def pooled_scores(b, i):
                h, t = divmod(i, MT)
                for half in range(2):
                    last = mm(slot[ST_SLOT[i]][:, half], ks[0:SM, h, t * P:(t + 1) * P], qs[0:SM, h, halves(half)],
                              True, True)
                last.then_inc(st_pe, 1)

            def by_head(s, lhsT, ready):
                for half in range(2):
                    for t in range(MT):
                        for h in range(HEADS):
                            last = mm(slot[s][HD * h:HD * (h + 1), half], lhsT(t, h), probs[:, h * MT + t, halves(half)],
                                      t == 0, t == MT - 1)
                    if ready is lden_pe or half == 1:
                        last.then_inc(ready, 1)

            def window_scores(b, to):
                for j in range(NW):
                    pe.wait_ge(prod_ready, b * NW + j + 1)
                    for half in range(2):
                        ins = mm(to[HD * j:HD * (j + 1), half], cst[:, C_HEAD:C_HEAD + HD], qk[:, j, halves(half)],
                                 True, True)
                ins.then_inc(ssum_pe, 1)

            def front(b, conv, first=False):
                pe.wait_ge(xhi_ready, (b + 1) * KT)
                pe.wait_ge(xlo_ready, (b + 1) * KT)
                project(0, WLQ)
                pe.wait_ge(pool_c, (b + 1) * N_POOL)
                if not first:
                    pe.wait_ge(y_ready, b * KT - 1)
                for k in range(KT):
                    split_mm(slot[1][:, 0, 0:G], (w_hi[:, k, WLK:WLK + P], w_lo[:, k, WLK:WLK + P]),
                             (pool_hi[:, k], pool_lo[:, k]), k == 0, k == KT - 1)
                for t in range(MT):
                    m = slice(t * P, (t + 1) * P)
                    for k in range(KT):
                        ins = split_mm(slot[1][:, 1, m], (pool_hi[:, k, m], pool_lo[:, k, m]),
                                       (w_hi[:, k, WLV:WLV + P], w_lo[:, k, WLV:WLV + P]), k == 0, k == KT - 1)
                ins.then_inc(proj_pe, 1)
                if not first:
                    pe.wait_ge(y_ready, b * KT)
                project(2, WQ)
                pe.wait_ge(lq_dve, b + 1)
                project(0, WK)
                conv.more(FRONT[0])
                if not first:
                    pe.wait_ge(qkv_sb, b * 3 + 1)
                    group_means(b - 1, 1)
                pe.wait_ge(lk_act, (b + 1) * 2)
                pe.wait_ge(lk_dve, b + 1)
                project(1, WV)
                conv.more(FRONT[1])
                for n in range(NB):
                    if n == 0:
                        pe.wait_ge(stacked, (b + 1) * STACK)
                        pe.wait_ge(qkv_sb, b * 3 + 2)
                    elif n == 1:
                        pe.wait_ge(qkv_sb, b * 3 + 3)
                    elif n == 2:
                        if not first:
                            pe.wait_ge(gn_c[1], (b - 1) * N_GN + GN_SENT + 1)
                    else:
                        pe.wait_ge(la_max, b * NB + n - 2)
                    for h in range(HEADS):
                        ins = mm(flat[LA_SLOT[n]][:, h * G:(h + 1) * G], qs[0:SC, h, n * P:(n + 1) * P], ks[0:SC, h],
                                 True, True)
                    ins.then_inc(la_pe, 1)
                    conv.more(FRONT[2 + n])
                if first:
                    window_scores(b, cps)
                pe.wait_ge(la_max, (b + 1) * NB)
                if first:
                    pe.wait_ge(zeroed_dve, 2)
                nc.tensor.transpose(slot[2][:, 0, 0:P], l_max[:], cst[:, C_ID:C_ID + P]).then_inc(lmt_pe, 1)

                conv.more(FRONT[10])
                if not first:
                    window_scores(b, slot[0])
                conv.more(FRONT[11])
                pe.wait_ge(ssum_sb, b + 1)
                pe.wait_ge(lm_dve, (b + 1) * 2)
                for n in range(NB):
                    ins = nc.tensor.transpose(slot[2][:, n // 4, (n % 4) * P:(n % 4 + 1) * P],
                                              q_w[:, n * P:(n + 1) * P], cst[:, C_ID:C_ID + P])
                ins.then_inc(stok_pe, 1)
                pe.wait_ge(max_stacked, (b + 1) * MAX_STACK)
                for i in range(2):
                    pooled_scores(b, i)
                conv.more(FRONT[12])

            def rest(b, first, last):
                conv = NoConvolution() if first else Convolution(b - 1)
                conv.more(REST[0])
                for i in range(2, LT - NW):
                    pe.wait_ge(st_exp, b * LT + i - 1)
                    pooled_scores(b, i)
                    conv.more(REST[1])
                pe.wait_ge(soft_c, (b + 1) * N_SOFT)
                for n in range(NB):
                    ins = nc.tensor.transpose(slot[2][:, n // 4, (n % 4) * P:(n % 4 + 1) * P],
                                              s_soft[:, n].rearrange("p j h -> p (j h)"), cst[:, C_ID:C_ID + P])
                ins.then_inc(pt_pe, 1)
                conv.more(REST[2])
                pe.wait_ge(pt_act, b + 1)
                for j in range(NW):
                    if j < 2:
                        pe.wait_ge(st_exp, b * LT + j + 3)
                    elif j == 3:
                        pe.wait_ge(pv_ready, b * NW + 1)
                    for half in range(2):
                        ins = mm(slot[PB_SLOT[j]][:, half], sel[:, j], p_w[:, halves(half)], True, True)
                    ins.then_inc(pb_pe, 1)
                    conv.more(REST[3])
                for i in range(LT - NW, LT):
                    if i < LT - 1:
                        pe.wait_ge(pv_ready, b * NW + i - 2)
                    else:
                        pe.wait_ge(st_exp, b * LT + 5)
                    pooled_scores(b, i)
                    conv.more(REST[4])
                if not last:
                    pe.wait_ge(st_exp, b * LT + LT - 2)
                    group_means(b + 1, 0)
                    pe.wait_ge(gn_c[0], (b + 1) * N_GN + GN_SENT + 1)
                pe.wait_ge(st_exp, (b + 1) * LT)
                by_head(2, lambda t, h: cst[:, C_ONE:C_ONE + HD], lden_pe)
                pe.wait_ge(pv_dve, (b + 1) * 2)
                for half in range(2):
                    ins = mm(slot[1][:, half], w_out[:, 0], q_w[:, halves(half)], True, True)
                ins.then_inc(out_pe, 1)
                by_head(0, lambda t, h: lv[:, t, HD * h:HD * (h + 1)], lpv_pe)
                conv.more(REST[5])
                pe.wait_ge(lnorm, b + 1)
                for half in range(2):
                    ins = mm(slot[2][:, half], w_out[:, 1], k_w[:, halves(half)], True, True)
                ins.then_inc(out_pe, 1)
                conv.more(PAIR - conv.at)
                return conv

            def step(b, first, last):
                conv = rest(b, first, last)
                if not last:
                    front(b + 1, conv)
                else:
                    conv.more(CONV_MM // 2)
                    pe.wait_ge(y_ready, B * KT)
                    group_means(b, 1)
                    conv.more(PAIR)

            pe.wait_ge(cst_in, 16)
            group_means(0, 0)
            pe.wait_ge(w_split, 2)
            pe.wait_ge(gn_c[0], N_GN)
            front(0, NoConvolution(), first=True)
            step(0, True, False)
            pe.wait_ge(cw_split, 4 * KT)
            with pe.Fori(1, B - 1) as b:
                step(b, False, False)
            step(B - 1, False, True)
            Convolution(B - 1).more(GROUPS * CONV_MM)


def constants():
    import numpy as np
    c, s = np.zeros((P, C_ALL), np.float32), np.zeros((P, SEL_COLS), np.float32)
    p = np.arange(P)
    c[:, C_ID:C_ID + P] = np.eye(P)
    c[:, C_GRP:C_GRP + P] = (p[:, None] // GROUP == p[None] // GROUP) / GROUP
    for h in range(HEADS):
        c[:, C_HEAD + h] = p // HD == h
    c[:, C_ONE:C_ONE + HD] = 1
    for j in range(NW):
        for part in range(2):
            s[:, j * P:(j + 1) * P] += p[:, None] == HD * j + HEADS * part + p[None] // HD
    c[:, C_IX:C_IX + H] = np.arange(1, H + 1)
    c[:, C_POS:C_POS + H] = np.linspace(-1, 1, H)
    return c, s


def kernel(x, L0_conv_h_qkv_w, L0_conv_h_proj_w, L0_conv_h_proj_b, L0_conv_l_q_w, L0_conv_l_kv_w, L0_conv_l_proj_w,
           L0_conv_l_proj_b, L1_conv_weight, L1_conv_bias, L1_conv_mask_weight, L1_conv_filter):
    import numpy as np
    import concourse.bacc as bacc
    from concourse.bass_utils import run_bass_kernel_spmd

    tiles = lambda a: np.ascontiguousarray(np.asarray(a).reshape(KT, P, -1))
    mixed = lambda a: np.asarray(a).reshape(C, HEADS, HD).transpose(0, 2, 1).reshape(C, P)
    cols = lambda a: np.ascontiguousarray(np.asarray(a).reshape(-1, P).T)
    arrays = {
        "x": np.ascontiguousarray(np.asarray(x).reshape(B, KT, P, HW)),
        "h_qkv": tiles(L0_conv_h_qkv_w), "l_q": tiles(mixed(L0_conv_l_q_w)),
        "l_kv": tiles(np.concatenate([mixed(L0_conv_l_kv_w[:, :P]), L0_conv_l_kv_w[:, P:]], 1)),
        "h_proj": np.ascontiguousarray(L0_conv_h_proj_w), "l_proj": np.ascontiguousarray(L0_conv_l_proj_w),
        "h_bias": cols(L0_conv_h_proj_b), "l_bias": cols(L0_conv_l_proj_b),
        "conv_w": tiles(np.asarray(L1_conv_weight).reshape(C, C, TAPS).transpose(1, 2, 0)),
        "conv_b": cols(L1_conv_bias), "mask_w": cols(L1_conv_mask_weight), "filt": cols(L1_conv_filter),
        "consts": constants()[0], "selectors": constants()[1],
    }
    nc = bacc.Bacc("TRN2", target_bir_lowering=False, num_devices=1)
    t = {n: nc.dram_tensor(n, a.shape, F32, kind="ExternalInput").ap() for n, a in arrays.items()}
    out = nc.dram_tensor("out", (B, KT, P, HW), F32, kind="ExternalOutput").ap()
    build(nc, t["x"], (t["h_qkv"], t["l_q"], t["l_kv"]), t["h_proj"], t["l_proj"], t["h_bias"], t["l_bias"],
          t["conv_w"], t["conv_b"], t["mask_w"], t["filt"], t["consts"], t["selectors"], out)
    r = run_bass_kernel_spmd(nc, [arrays], core_ids=[0])
    return np.asarray(r.results[0]["out"]).reshape(B, C, H, W)
```

```python
from contextlib import ExitStack

import concourse.bass as bass
from concourse import mybir

F32 = mybir.dt.float32
F32R = mybir.dt.float32r
I32 = mybir.dt.int32
ALU = mybir.AluOpType
ACT = mybir.ActivationFunctionType
AX_X = mybir.AxisListType.X

P = 128
B, C, H, W = 4, 256, 32, 32
KT = C // P
HW = H * W
WS = 2
NW = WS * WS
HG, WG = H // WS, W // WS
G = HG * WG
HALF = 512
HEADS, HD = 4, 32
SCALE = HD ** -0.5
MT = G // P
LT = HEADS * MT
SC = 3 * HD
SM = SC + 2
NB = HW // P
TAPS = 9
PADW = W + 2
GROUP = 8
EPS = 1e-5
ROUND = 12582912.0
MAGIC = 0x5F3759DF
IX_SUM = float(W * H * (H + 1) // 2)
LIN = 2.0 / (H - 1)

C_ID, C_GRP, C_HEAD, C_ONE = 0, P, 2 * P, 2 * P + HD
C_IX = C_ONE + HD
C_POS = C_IX + H
C_ALL = C_POS + H
SEL_COLS = NW * P

WQ, WK, WV, WLQ, WLK, WLV = (P * i for i in range(6))
WCOLS = 6 * P

LA_SLOT = (0, 1, 2, 0, 1, 2, 0, 1)
ST_SLOT = (0, 1, 0, 1, 1, 0, 2, 1)
PB_SLOT = (0, 1, 0, 2)

GROUPS = 2 * KT
CONV_MM = KT * TAPS * 3
PAIR = 2 * CONV_MM
TAP_ORDER = (4, 0, 1, 2, 3, 5, 6, 7, 8)

EARLY = 12
REST = (6, 4, 8, 4, 6, 12)
FRONT = (0, 10, 0, 0, 15, 5, 30, 6, 6, 8, 4, 12, 12)
WARM = (5, 0, 0, 0, 0, 0, 6, 1, 2, 4, 4)

N_GN, N_MASK, N_SOFT, N_POOL = 20, 17, 7, 4
GN_SENT, SOFT_READ = 4, 2


def wait_count(eng, sem, n):
    if not (isinstance(n, int) and n <= 0):
        eng.wait_ge(sem, n)


class Chain:

    def __init__(self, eng, sem, length, image):
        self.eng, self.sem, self.base, self.length, self.n = eng, sem, image * length, length, 0

    def __call__(self, ins):
        self.n += 1
        ins.then_inc(self.sem, 1)
        if self.n < self.length:
            self.eng.wait_ge(self.sem, self.base + self.n)


def build(nc, x, wqkv, whp, wlp, bh, bl, cw, cb, mw, filt, consts, selectors, out):
    with ExitStack() as ctx:
        def sb(name, shape, dt=F32):
            return ctx.enter_context(nc.sbuf_tensor(name, shape, dt))

        def sem(name):
            return ctx.enter_context(nc.semaphore(name))

        xy = sb("xy", [P, B * KT * HW])
        cst = sb("cst", [P, C_ALL])
        sel = sb("sel", [P, NW, P], F32R)
        w_hi = sb("w_hi", [P, KT, WCOLS], F32R)
        w_lo = sb("w_lo", [P, KT, WCOLS], F32R)
        w_out = sb("w_out", [P, 2, P])
        bias = sb("bias", [P, 2])
        cw_hi = sb("cw_hi", [P, KT * TAPS * C], F32R)
        cw_lo = sb("cw_lo", [P, KT * TAPS * C], F32R)
        cbias = sb("cbias", [P, KT])
        mwf = sb("mwf", [P, 3, KT])
        xn = sb("xn", [P, KT, HW])
        xn_hi = sb("xn_hi", [P, KT, HW], F32R)
        xn_lo = sb("xn_lo", [P, KT, HW], F32R)
        p_w = xn_lo[:, 0]
        pool_hi = sb("pool_hi", [P, KT, G], F32R)
        pool_lo = sb("pool_lo", [P, KT, G], F32R)
        q_w = sb("q_w", [P, HW])
        k_w = sb("k_w", [P, HW])
        v_w = sb("v_w", [P, HW])
        qs = sb("qs", [P, HEADS, HW], F32R)
        ks = sb("ks", [P, HEADS, G], F32R)
        lv = sb("lv", [P, MT, P])
        probs = sb("probs", [P, LT, HW])
        qk = probs[:, LT - NW:LT, :]
        pv = (q_w[:], k_w[:], xn[:, 0], xn[:, 1])
        lq_hi, lq_lo = probs[:, 0].bitcast(F32R), probs[:, 1]
        lk_hi, lk_lo = probs[:, 2, 0:G].bitcast(F32R), probs[:, 2, G:2 * G]
        lm_hi, lm_lo = probs[0:NB * HEADS, 3, 0:P].bitcast(F32R), probs[0:NB * HEADS, 3, P:2 * P]
        raw = qk.rearrange("p a b -> p (a b)")
        raw_w = raw[:, 0:KT * WCOLS].rearrange("p (k n) -> p k n", k=KT)
        raw_sel = raw[:, KT * WCOLS:KT * WCOLS + SEL_COLS]
        s_soft = k_w[:].rearrange("p (n j r) -> p n j r", n=NB, j=NW)
        s_exp, s_hi = s_soft[:, :, :, 0:HEADS], s_soft[:, :, :, HEADS:2 * HEADS]
        s_max = sb("s_max", [P, NB, HEADS])
        s_den = sb("s_den", [P, NB, HEADS])
        l_max = sb("l_max", [P, P])
        im_hi = sb("im_hi", [P, KT, H, PADW], F32R)
        im_lo = sb("im_lo", [P, KT, H, PADW], F32R)
        mask = sb("mask", [P, KT, HW])
        pool_t, pool_s = mask[:, :, 0:2 * G], mask[:, :, 2 * G:3 * G]
        first_taps = (TAPS - 1) * C
        raw_cw = [((0, first_taps), xy[:, (B - KT + k) * KT * HW:][:, 0:first_taps]) for k in range(KT)]
        raw_cw = [(raw_cw[k], ((first_taps, TAPS * C), mask[:, k, 3 * G:])) for k in range(KT)]
        st = [sb(f"st{i}", [P, KT, 2, 6]) for i in range(2)]
        mv = [sb(f"mv{i}", [P, KT, 2]) for i in range(2)]
        gn = [sb(f"gn{i}", [P, 8, KT]) for i in range(2)]
        rc = sb("rc", [P, KT, 2, H])
        rw = sb("rw", [P, KT, 2, H])
        mu = sb("mu", [P, KT, 2])
        idle = sb("idle", [P, 1])
        sx = gn[1][:, 2:4]

        cps = ctx.enter_context(nc.psum_tensor("cps", [P, 2, HALF], F32))
        slot = [ctx.enter_context(nc.psum_tensor(f"slot{i}", [P, 2, HALF], F32)) for i in range(3)]
        *flat, flat_cps = [s[:].rearrange("p a b -> p (a b)") for s in (*slot, cps)]

        x_in = [[sem(f"x_in0_{k}") for k in range(KT)]] + [sem(f"x_in{b}") for b in range(1, B)]
        w_in, cw_in, c_in, cst_in = sem("w_in"), sem("cw_in"), sem("c_in"), sem("cst_in")
        w_split = sem("w_split")
        out_done = sem("out_done")
        w_ready = sem("w_ready")
        cw_split = sem("cw_split")
        zeroed = sem("zeroed")
        im_free = sem("im_free")
        ones = sem("ones")
        gn_c = [sem("gn1_c"), sem("gn2_c")]
        gn_pe = [sem("gn1_pe"), sem("gn2_pe")]
        mask_c, soft_c, pool_c = sem("mask_c"), sem("soft_c"), sem("pool_c")
        xhi_ready, xn_ready = sem("xhi_ready"), sem("xn_ready")
        xlo_ready = sem("xlo_ready")
        proj_pe = sem("proj_pe")
        qkv_sb = sem("qkv_sb")
        lq_act, lq_dve = sem("lq_act"), sem("lq_dve")
        lk_act, lk_dve = sem("lk_act"), sem("lk_dve")
        stacked, max_stacked = sem("stacked"), sem("max_stacked")
        prod_ready = sem("prod_ready")
        ssum_pe, ssum_sb = sem("ssum_pe"), sem("ssum_sb")
        stok_pe, sexp = sem("stok_pe"), sem("sexp")
        pt_pe, pt_act = sem("pt_pe"), sem("pt_act")
        la_pe, la_max = sem("la_pe"), sem("la_max")
        lmt_pe, lm_dve = sem("lmt_pe"), sem("lm_dve")
        pb_pe, pv_ready = sem("pb_pe"), sem("pv_ready")
        pv_pool, pv_dve = sem("pv_pool"), sem("pv_dve")
        st_pe, st_exp = sem("st_pe"), sem("st_exp")
        lden_pe, linv = sem("lden_pe"), sem("linv")
        lpv_pe, lnorm = sem("lpv_pe"), sem("lnorm")
        out_pe, y_ready = sem("out_pe"), sem("y_ready")
        yn_ready = sem("yn_ready")
        msum, masked = sem("msum"), sem("masked")
        im_act, im_dve = sem("im_act"), sem("im_dve")
        conv_pe, conv_out = sem("conv_pe"), sem("conv_out")

        block = ctx.enter_context(nc.Block())

        def img(b, k, lo=0, n=HW):
            return xy[:, bass.ds(b * (KT * HW) + (k * HW + lo), n)]

        def run(eng, step):
            step(0, True, False)
            with eng.Fori(1, B - 1) as b:
                step(b, False, False)
            step(B - 1, False, True)

        @block.sync
        def _(sp):
            def load(b):
                for k in range(KT):
                    sp.dma_start(img(b, k), x[b, k]).then_inc(x_in[b] if b else x_in[0][k], 16)

            load(0)
            sp.dma_start(cst[:], consts).then_inc(cst_in, 16)
            for c0, src in zip((WQ, WLQ, WLK), wqkv):
                for k in range(KT):
                    sp.dma_start(raw_w[:, k, c0:c0 + src.shape[2]], src[k]).then_inc(w_in, 16)
            for dst, src in ((raw_sel, selectors), (w_out[:, 0], whp), (w_out[:, 1], wlp), (bias[:, 0:1], bh),
                             (bias[:, 1:2], bl), (cbias[:], cb), (mwf[:, 0], mw), (mwf[:, 1], filt)):
                sp.dma_start(dst, src).then_inc(c_in, 16)

            def store(b, o, count):
                sp.wait_ge(conv_out, count)
                sp.dma_start(out[bass.ds(b, 1), o].rearrange("b p n -> p (b n)"), img(b, o)).then_inc(out_done, 16)

            def stack(count, count_k):
                def rows(to, part, parts):
                    sp.dma_start(to[HD * part:HD * (part + 1)].bitcast(F32), parts.bitcast(F32)).then_inc(stacked, 16)

                sp.wait_ge(lq_act, count)
                rows(qs, 0, lq_hi)
                rows(qs, 2, lq_hi)
                sp.wait_ge(lq_dve, count)
                rows(qs, 1, lq_lo)
                sp.wait_ge(lk_act, count_k)
                rows(ks, 0, lk_hi)
                rows(ks, 1, lk_hi)
                sp.wait_ge(lk_dve, count)
                rows(ks, 2, lk_lo)

            def stack_maxima(count):
                sp.wait_ge(lm_dve, count)
                for i, t in enumerate((lm_hi, lm_lo)):
                    sp.dma_start(qs[SC + i:SC + i + 1].bitcast(F32), t.bitcast(F32)).then_inc(max_stacked, 16)

            def step(b, first, last):
                counts = (b - 1, (b + 1) * GROUPS - 2, (b + 1) * GROUPS, b + 2, b * 2 + 3, b * 2 + 4)
                if not (first or last):
                    counts = [sp.snap(n) for n in counts]
                prev, tile_0, tile_1, parts, parts_k, parts_max = counts
                if first:
                    for k in range(KT):
                        sp.wait_ge(cw_split, 2 * KT + 2 * (k + 1))
                        load(B - KT + k)
                else:
                    store(prev, 0, tile_0)
                if not last:
                    stack(parts, parts_k)
                    stack_maxima(parts_max)
                if not first:
                    store(prev, 1, tile_1)

            stack(1, 1)
            load(1)
            for k in range(KT):
                for (c0, c1), to in raw_cw[k]:
                    sp.dma_start(to, cw[k][:, c0:c1]).then_inc(cw_in, 16)
            stack_maxima(2)
            run(sp, step)
            for g in range(GROUPS):
                o, half = divmod(g, 2)
                h = slice(half * HALF, (half + 1) * HALF)
                sp.wait_ge(conv_out, B * GROUPS + g + 1)
                sp.dma_start(out[B - 1, o][:, h], img(B - 1, o, half * HALF, HALF)).then_inc(out_done, 16)
            sp.wait_ge(out_done, ((B - 1) * KT + GROUPS) * 16)

        CONST_LOADS = 8 * 16
        STACK, MAX_STACK = 6 * 16, 2 * 16

        @block.gpsimd
        def _(pool):
            def mask_sum(b, pooled):
                pool.wait_ge(mask_c, (b + 1) * N_MASK)
                pool.wait_ge(pool_c, pooled * N_POOL)
                for k in range(KT):
                    nc.gpsimd.tensor_tensor(mask[:, k].rearrange("p (h w) -> p h w", h=H),
                                            rw[:, k, 0].unsqueeze(2).to_broadcast([P, H, W]),
                                            rw[:, k, 1].unsqueeze(1).to_broadcast([P, H, W]),
                                            ALU.add).then_inc(msum, 1)

            def products(b, keys):
                for j in keys:
                    nc.gpsimd.tensor_tensor(
                        qk[:, j].rearrange("p (n w) -> p n w", n=NW),
                        q_w[:].rearrange("p (n w) -> p n w", n=NW),
                        k_w[:, j * G:(j + 1) * G].unsqueeze(1).to_broadcast([P, NW, G]),
                        ALU.mult).then_inc(prod_ready, 1)

            def split_conv_weights():
                pool.wait_ge(cw_in, 2 * KT * 16)
                pieces = [(k * TAPS * C, cols, src) for k in range(KT) for cols, src in raw_cw[k]]
                for base, (c0, c1), src in pieces:
                    nc.gpsimd.tensor_scalar(cw_hi[:, base + c0:base + c1], src, 1.0, 0.0, ALU.mult,
                                            ALU.add).then_inc(cw_split, 1)
                for i, (base, (c0, c1), src) in enumerate(pieces):
                    pool.wait_ge(cw_split, 2 * KT + i)
                    nc.gpsimd.tensor_tensor(cw_lo[:, base + c0:base + c1], src, cw_hi[:, base + c0:base + c1].bitcast(F32),
                                            ALU.subtract).then_inc(cw_split, 1)

            def step(b, first, last):
                pool.wait_ge(qkv_sb, b * 3 + 2)
                wait_count(pool, lpv_pe, b)
                products(b, range(NW))
                if first:
                    split_conv_weights()
                else:
                    mask_sum(b - 1, b + 1)
                pool.wait_ge(pv_ready, b * NW + 2)
                nc.gpsimd.tensor_tensor(pv[0], pv[0], pv[1], ALU.add).then_inc(pv_pool, 1)

            nc.gpsimd.memset(l_max[:], 0.0).then_inc(zeroed, 1)
            for i, t in enumerate((im_hi, im_lo)):
                pool.wait_ge(zeroed, i + 1)
                nc.gpsimd.memset(t[:].rearrange("p k h w -> p (k h w)").bitcast(F32), 0.0).then_inc((zeroed, im_free)[i], 1)
            pool.wait_ge(w_split, 1)
            nc.gpsimd.tensor_tensor(w_lo[:], raw_w, w_hi[:].bitcast(F32), ALU.subtract).then_inc(w_split, 1)
            pool.wait_ge(w_split, 2)
            pool.wait_ge(w_ready, 3)
            run(pool, step)
            mask_sum(B - 1, B)

        @block.scalar
        def _(act):
            def normalise(b, first=False):
                act.wait_ge(gn_c[0], (b + 1) * N_GN)
                wait_count(act, xlo_ready, b * KT)
                wait_count(act, pool_c, b * N_POOL)
                wait_count(act, pv_dve, b * 2)
                for k in range(KT):
                    src = img(b, k).rearrange("p (hg a wg b) -> p a b hg wg", hg=HG, a=WS, wg=WG, b=WS)
                    for t, ready in ((xn_hi, xhi_ready), (xn, xn_ready))[0:1 if first else 2]:
                        dst = t[:, k].rearrange("p (a b hg wg) -> p a b hg wg", a=WS, b=WS, hg=HG)
                        for a in range(WS):
                            last = nc.scalar.activation(dst[:, a], src[:, a], ACT.Identity,
                                                        bias=gn[0][:, 6, k:k + 1], scale=gn[0][:, 5, k:k + 1])
                        last.then_inc(ready, 1)

            def projections(b, first):
                wait_count(act, lpv_pe, b)
                act.wait_ge(proj_pe, b * 5 + 1)
                nc.scalar.copy(lq_hi, flat[0]).then_inc(lq_act, 1)
                act.wait_ge(proj_pe, b * 5 + 2)
                nc.scalar.copy(lk_hi, slot[1][:, 0, 0:G]).then_inc(lk_act, 1)
                nc.scalar.activation(lv[:].rearrange("p a b -> p (a b)"), slot[1][:, 1, 0:MT * P], ACT.Copy,
                                     scale=1.0 / NW).then_inc(lk_act, 1)
                wait_count(act, y_ready, b * KT)
                for i, (src, dst) in enumerate(((flat[2], q_w), (flat[0], k_w), (flat_cps if first else flat[1], v_w))):
                    act.wait_ge(proj_pe, b * 5 + i + 3)
                    nc.scalar.copy(dst[:], src).then_inc(qkv_sb, 1)

            def normalise_y(b, normalised):
                act.wait_ge(gn_c[1], (b + 1) * N_GN)
                act.wait_ge(xlo_ready, normalised * KT)
                act.wait_ge(pool_c, normalised * N_POOL)
                for k in range(KT):
                    nc.scalar.activation(xn[:, k], img(b, k), ACT.Identity, bias=gn[1][:, 6, k:k + 1],
                                         scale=gn[1][:, 5, k:k + 1]).then_inc(yn_ready, 1)

            def conv_input(b, k):
                act.wait_ge(masked, b * KT + k + 1)
                nc.scalar.activation(im_hi[:, k, :, 1:W + 1], mask[:, k].rearrange("p (h w) -> p h w", h=H),
                                     ACT.Relu).then_inc(im_act, 1)

            def exp_scores(b, tiles):
                for i in tiles:
                    act.wait_ge(st_pe, b * LT + i + 1)
                    nc.scalar.activation(probs[:, i], flat[ST_SLOT[i]], ACT.Exp, scale=SCALE / NW)\
                        .then_inc(st_exp, 1)

            def step(b, first, last):
                if first:
                    act.wait_ge(w_in, 3 * KT * 16)
                    nc.scalar.copy(w_hi[:], raw_w).then_inc(w_split, 1)
                    normalise(b, first=True)
                projections(b, first)
                if not first:
                    normalise_y(b - 1, b + 1)
                    conv_input(b - 1, 0)
                act.wait_ge(ssum_pe, b + 1)
                nc.scalar.copy(q_w[:], flat_cps if first else flat[0]).then_inc(ssum_sb, 1)
                act.wait_ge(soft_c, b * N_SOFT + SOFT_READ)
                nc.scalar.activation(s_exp, s_exp, ACT.Exp, scale=SCALE).then_inc(sexp, 1)
                exp_scores(b, range(2))
                if not first:
                    conv_input(b - 1, 1)
                exp_scores(b, range(2, LT - NW))
                act.wait_ge(pt_pe, b + 1)
                nc.scalar.copy(p_w, flat[2]).then_inc(pt_act, 1)
                exp_scores(b, range(LT - NW, LT))
                if not last:
                    normalise(b + 1)

            run(act, step)
            normalise_y(B - 1, B)
            for k in range(KT):
                conv_input(B - 1, k)

        @block.vector
        def _(dve):
            class Statistics:

                def __init__(self, b, i):
                    self.b, self.i = b, i
                    self.link = Chain(dve, gn_c[i], N_GN, b)

                def of_channels(self):
                    link, s, m, g = self.link, st[self.i], mv[self.i], gn[self.i]
                    for k in range(KT):
                        if isinstance(self.b, int) and self.b == 0 and self.i == 0:
                            dve.wait_ge(x_in[0][k], 16)
                        for half in range(2):
                            last = nc.vector.bn_stats(s[:, k, half], img(self.b, k, half * HALF, HALF))
                    link(last)
                    nc.vector.memset(g[:, 7], 0.0)
                    for k in range(KT):
                        last = nc.vector.bn_aggr(m[:, k], s[:, k].rearrange("p a b -> p (a b)"))
                    link(last)
                    link(nc.vector.tensor_tensor(g[:, 2], m[:, :, 0], m[:, :, 0], ALU.mult))
                    link(nc.vector.tensor_tensor(m[:, :, 1], m[:, :, 1], g[:, 2], ALU.add))

                def of_groups(self):
                    dve.wait_ge(gn_pe[self.i], self.b + 1)
                    src = slot[2][:, 0, 0:2 * KT].rearrange("p (k s) -> p s k", s=2)
                    self.link(nc.vector.tensor_copy(gn[self.i][:, 0:2], src))

                def scale_and_bias(self):
                    link, g = self.link, gn[self.i]
                    link(nc.vector.tensor_tensor(g[:, 2], g[:, 0], g[:, 0], ALU.mult))
                    link(nc.vector.scalar_tensor_tensor(g[:, 3], g[:, 1], EPS, g[:, 2], ALU.add, ALU.subtract))
                    link(nc.vector.tensor_scalar(g[:, 4], g[:, 3], -0.5, None, ALU.mult))
                    link(nc.vector.tensor_scalar(g[:, 7].bitcast(I32), g[:, 3].bitcast(I32), 1, None,
                                                 ALU.logical_shift_right))
                    link(nc.vector.tensor_scalar(g[:, 5].bitcast(I32), g[:, 7].bitcast(I32), -1.0, float(MAGIC),
                                                 ALU.mult, ALU.add))
                    for _ in range(3):
                        link(nc.vector.tensor_tensor(g[:, 7], g[:, 5], g[:, 5], ALU.mult))
                        link(nc.vector.tensor_tensor(g[:, 7], g[:, 7], g[:, 4], ALU.mult))
                        link(nc.vector.scalar_tensor_tensor(g[:, 5], g[:, 7], 1.5, g[:, 5], ALU.add, ALU.mult))
                    link(nc.vector.scalar_tensor_tensor(g[:, 6], g[:, 0], -1.0, g[:, 5], ALU.mult, ALU.mult))
                    assert link.n == N_GN

            def split_input(b, tiles=range(KT)):
                wait_count(dve, proj_pe, b * 5)
                for k in tiles:
                    dve.wait_ge(xhi_ready, b * KT + k + 1)
                    dve.wait_ge(xn_ready, b * KT + k + 1)
                    nc.vector.tensor_tensor(xn_lo[:, k], xn[:, k], xn_hi[:, k].bitcast(F32),
                                            ALU.subtract).then_inc(xlo_ready, 1)

            def pooling(b):
                link = Chain(dve, pool_c, N_POOL, b)
                link(nc.vector.tensor_tensor(pool_t, xn[:, :, 0:2 * G], xn[:, :, 2 * G:4 * G], ALU.add))
                link(nc.vector.tensor_tensor(pool_s, pool_t[:, :, 0:G], pool_t[:, :, G:2 * G], ALU.add))
                link(nc.vector.tensor_copy(pool_hi[:], pool_s))
                link(nc.vector.tensor_tensor(pool_lo[:], pool_s, pool_hi[:].bitcast(F32), ALU.subtract))

            def line_sums(b):
                carry()
                y = xy[:, bass.ds(b * (KT * HW), KT * HW)]
                nc.vector.tensor_reduce(rc[:, :, 0], y.rearrange("p (k h w) -> p k h w", k=KT, h=H), AX_X, ALU.add)
                nc.vector.tensor_reduce(rc[:, :, 1], y.rearrange("p (k h w) -> p k w h", k=KT, h=H), AX_X,
                                        ALU.add).then_inc(mask_c, 1)

            def mask_parts(b):
                link = Chain(dve, mask_c, N_MASK, b)
                link.n = 1
                dve.wait_ge(mask_c, b * N_MASK + 1)
                g = gn[1]
                both = [t[:].rearrange("p k s n -> p (k s) n") for t in (rc, rw)]
                m4 = mu[:].rearrange("p k s -> p (k s)")
                link(nc.vector.tensor_tensor(both[1], both[0],
                                             cst[:, C_IX:C_IX + H].unsqueeze(1).to_broadcast([P, 2 * KT, H]), ALU.mult))
                link(nc.vector.tensor_reduce(m4, both[1], AX_X, ALU.add))
                link(nc.vector.tensor_tensor(sx[:, 0], mv[1][:, :, 0], g[:, 0], ALU.subtract))
                link(nc.vector.scalar_tensor_tensor(sx[:, 0], sx[:, 0], float(HW), g[:, 5], ALU.mult, ALU.mult))
                link(nc.vector.tensor_scalar(sx[:, 0], sx[:, 0], 1e-9, None, ALU.max))
                link(nc.vector.reciprocal(sx[:, 1], sx[:, 0]))
                link(nc.vector.tensor_tensor(sx[:, 1], sx[:, 1], g[:, 5], ALU.mult))
                link(nc.vector.scalar_tensor_tensor(mu[:], g[:, 0].unsqueeze(2).to_broadcast([P, KT, 2]), -IX_SUM,
                                                    mu[:], ALU.mult, ALU.add))
                link(nc.vector.tensor_tensor(mu[:], mu[:], sx[:, 1].unsqueeze(2).to_broadcast([P, KT, 2]), ALU.mult))
                link(nc.vector.tensor_scalar(m4, m4, 1.0, float(H), ALU.max, ALU.min))
                link(nc.vector.tensor_scalar(m4, m4, ROUND, -ROUND, ALU.add, ALU.add))
                link(nc.vector.tensor_scalar(m4, m4, LIN, -1.0 - LIN, ALU.mult, ALU.add))
                link(nc.vector.tensor_tensor(both[0], cst[:, C_POS:C_POS + H].unsqueeze(1).to_broadcast([P, 2 * KT, H]),
                                             m4.unsqueeze(2).to_broadcast([P, 2 * KT, H]), ALU.subtract))
                link(nc.vector.scalar_tensor_tensor(both[1], both[0], -1.0, both[0], ALU.mult, ALU.max))
                link(nc.vector.tensor_tensor(rw[:].rearrange("p k s n -> p k (s n)"),
                                             rw[:].rearrange("p k s n -> p k (s n)"),
                                             mwf[:, 2].unsqueeze(2).to_broadcast([P, KT, 2 * H]), ALU.mult))
                link(nc.vector.tensor_scalar(rw[:, :, 0], rw[:, :, 0], 1.0, None, ALU.add))
                assert link.n == N_MASK

            def masked_image(b, k):
                if k == 0:
                    dve.wait_ge(im_free, b + 1)
                dve.wait_ge(msum, b * KT + k + 1)
                dve.wait_ge(yn_ready, b * KT + k + 1)
                nc.vector.scalar_tensor_tensor(mask[:, k], mask[:, k], -1.0, xn[:, k], ALU.max,
                                               ALU.mult).then_inc(masked, 1)

            def image_lo(b, k):
                dve.wait_ge(im_act, b * KT + k + 1)
                nc.vector.scalar_tensor_tensor(im_lo[:, k, :, 1:W + 1], mask[:, k].rearrange("p (h w) -> p h w", h=H), 0.0,
                                               im_hi[:, k, :, 1:W + 1].bitcast(F32), ALU.max,
                                               ALU.subtract).then_inc(im_dve, 1)

            def query_lo(b):
                dve.wait_ge(lq_act, b + 1)
                nc.vector.tensor_tensor(lq_lo, flat[0], lq_hi.bitcast(F32), ALU.subtract).then_inc(lq_dve, 1)

            def key_lo(b):
                dve.wait_ge(lk_act, b * 2 + 2)
                nc.vector.tensor_tensor(lk_lo, slot[1][:, 0, 0:G], lk_hi.bitcast(F32), ALU.subtract).then_inc(lk_dve, 1)

            def maxima(b, blocks):
                for n in blocks:
                    dve.wait_ge(la_pe, b * NB + n + 1)
                    nc.vector.tensor_reduce(l_max[:, bass.ds(n, HEADS, step=NB)],
                                            flat[LA_SLOT[n]].rearrange("p (h m) -> p h m", h=HEADS), AX_X, ALU.max,
                                            negate=True).then_inc(la_max, 1)

            def maxima_parts(b):
                dve.wait_ge(lmt_pe, b + 1)
                rows = slot[2][0:NB * HEADS, 0, 0:P]
                nc.vector.tensor_copy(lm_hi, rows).then_inc(lm_dve, 1)
                dve.wait_ge(lm_dve, b * 2 + 1)
                nc.vector.tensor_tensor(lm_lo, rows, lm_hi.bitcast(F32), ALU.subtract).then_inc(lm_dve, 1)

            def window_softmax(b):
                link = Chain(dve, soft_c, N_SOFT, b)
                dve.wait_ge(stok_pe, b + 1)
                s = flat[2].rearrange("p (n j h) -> p n j h", n=NB, j=NW)[:, :, :, 0:HEADS]
                e = s_exp
                link(nc.vector.tensor_reduce(s_max[:], s.rearrange("p n j h -> p n h j"), AX_X, ALU.max))
                link(nc.vector.tensor_tensor(e, s, s_max[:].unsqueeze(2).to_broadcast([P, NB, NW, HEADS]), ALU.subtract))
                dve.wait_ge(sexp, b + 1)
                link(nc.vector.tensor_reduce(s_den[:], e.rearrange("p n j h -> p n h j"), AX_X, ALU.add))
                link(nc.vector.reciprocal(s_max[:], s_den[:]))
                link(nc.vector.tensor_tensor(e, e, s_max[:].unsqueeze(2).to_broadcast([P, NB, NW, HEADS]), ALU.mult))
                link(nc.vector.tensor_copy(s_hi.bitcast(F32R), e))
                link(nc.vector.tensor_tensor(e, e, s_hi, ALU.subtract))

            def conv_result(b, groups):
                for g in groups:
                    o, half = divmod(g, 2)
                    dve.wait_ge(conv_pe, b * GROUPS + g + 1)
                    dst = img(b, o, half * HALF, HALF)
                    nc.vector.scalar_tensor_tensor(dst, cps[:, g % 2], cbias[:, o:o + 1], dst, ALU.add,
                                                   ALU.add).then_inc(conv_out, 1)

            def residual(b, k, s):
                dve.wait_ge(out_pe, b * 2 + k + 1)
                y = img(b, k).rearrange("p (hg a wg b) -> p a b hg wg", hg=HG, a=WS, wg=WG, b=WS)
                for n in range(NW):
                    dst = y[:, n // WS, n % WS]
                    last = nc.vector.scalar_tensor_tensor(
                        dst, flat[s][:, n * G:(n + 1) * G].rearrange("p (hg wg) -> p hg wg", hg=HG),
                        bias[:, k:k + 1], dst, ALU.add, ALU.add)
                last.then_inc(y_ready, 1)

            def carry():
                nc.vector.memset(idle[:], 0.0)

            def masks(b, meanwhile=lambda: None):
                dve.wait_ge(y_ready, (b + 1) * KT)
                carry()
                stats = Statistics(b, 1)
                stats.of_channels()
                meanwhile()
                line_sums(b)
                stats.of_groups()
                stats.scale_and_bias()

            def front(b, older=None, first=False):
                query_lo(b)
                if first:
                    key_lo(b)
                else:
                    masks(b - 1, lambda: key_lo(b))
                maxima(b, range(3))
                if not first:
                    mask_parts(b - 1)
                maxima(b, range(3, 5))
                if not first:
                    masked_image(b - 1, 0)
                maxima(b, range(5, 6))
                if not first:
                    image_lo(b - 1, 0)
                maxima(b, range(6, NB))
                maxima_parts(b)
                window_softmax(b)
                if older is not None:
                    conv_result(older, (2, 3))
                if not first:
                    masked_image(b - 1, 1)
                    image_lo(b - 1, 1)

            def step(b, first, last):
                if first:
                    dve.wait_ge(x_in[1], KT * 16)
                if not last:
                    stats = Statistics(b + 1, 0)
                    stats.of_channels()
                for j in range(NW):
                    if j == 2 and not last:
                        stats.of_groups()
                    dve.wait_ge(pb_pe, b * NW + j + 1)
                    nc.vector.tensor_tensor(
                        pv[j].rearrange("p (n w) -> p n w", n=NW),
                        flat[PB_SLOT[j]].rearrange("p (n w) -> p n w", n=NW),
                        v_w[:, j * G:(j + 1) * G].unsqueeze(1).to_broadcast([P, NW, G]),
                        ALU.mult).then_inc(pv_ready, 1)
                dve.wait_ge(pv_ready, (b + 1) * NW)
                nc.vector.tensor_tensor(pv[2], pv[2], pv[3], ALU.add).then_inc(pv_dve, 1)
                dve.wait_ge(pv_dve, b * 2 + 1)
                dve.wait_ge(pv_pool, b + 1)
                nc.vector.tensor_tensor(q_w[:], pv[0], pv[2], ALU.add).then_inc(pv_dve, 1)
                if not last:
                    stats.scale_and_bias()
                for half in range(2):
                    h = slice(half * HALF, (half + 1) * HALF)
                    dve.wait_ge(lden_pe, b * 2 + half + 1)
                    nc.vector.reciprocal(v_w[:, h], flat[2][:, h]).then_inc(linv, 1)
                residual(b, 0, 1)
                dve.wait_ge(linv, (b + 1) * 2)
                dve.wait_ge(lpv_pe, b + 1)
                nc.vector.tensor_tensor(k_w[:], flat[0], v_w[:], ALU.mult).then_inc(lnorm, 1)
                if not last:
                    split_input(b + 1)
                residual(b, 1, 2)
                if not last:
                    pooling(b + 1)
                if not first:
                    conv_result(b - 1, (0, 1))
                if first:
                    for i in range(B - KT, B):
                        dve.wait_ge(x_in[i], KT * 16)
                if last:
                    masks(b)
                else:
                    front(b + 1, None if first else b - 1)

            stats = Statistics(0, 0)
            stats.of_channels()
            stats.of_groups()
            stats.scale_and_bias()
            dve.wait_ge(gn_c[0], N_GN)
            for k in range(KT):
                src = img(0, k).rearrange("p (hg a wg b) -> p a b hg wg", hg=HG, a=WS, wg=WG, b=WS)
                dst = xn[:, k].rearrange("p (a b hg wg) -> p a b hg wg", a=WS, b=WS, hg=HG)
                for a in range(WS):
                    ins = nc.vector.tensor_scalar(dst[:, a], src[:, a], gn[0][:, 5, k:k + 1], gn[0][:, 6, k:k + 1],
                                                  ALU.mult, ALU.add)
                ins.then_inc(xn_ready, 1)
                split_input(0, (k,))
            pooling(0)
            dve.wait_ge(c_in, CONST_LOADS)
            nc.vector.tensor_copy(sel[:].rearrange("p a b -> p (a b)"), raw_sel).then_inc(w_ready, 1)
            nc.vector.memset(idle[:], 0.0).then_inc(conv_out, GROUPS)
            nc.vector.memset(ks[SC:SM].bitcast(F32), 1.0).then_inc(ones, 1)
            nc.vector.scalar_tensor_tensor(mwf[:, 2], mwf[:, 1], 1.0, mwf[:, 0], ALU.is_equal,
                                           ALU.mult).then_inc(w_ready, 1)
            dve.wait_ge(w_ready, 2)
            nc.vector.tensor_scalar(mwf[:, 2], mwf[:, 2], -1.0, None, ALU.mult).then_inc(w_ready, 1)
            dve.wait_ge(w_ready, 3)
            front(0, first=True)
            run(dve, step)
            mask_parts(B - 1)
            masked_image(B - 1, 0)
            image_lo(B - 1, 0)
            conv_result(B - 2, (2, 3))
            masked_image(B - 1, 1)
            image_lo(B - 1, 1)
            conv_result(B - 1, range(GROUPS))

        @block.tensor
        def _(pe):
            def mm(dst, lhsT, rhs, start, stop):
                return nc.tensor.matmul(dst, lhsT, rhs, start=start, stop=stop)

            def split_mm(dst, lhsT, rhs, start=True, stop=True):
                mm(dst, lhsT[0], rhs[0], start, False)
                mm(dst, lhsT[0], rhs[1], False, False)
                return mm(dst, lhsT[1], rhs[0], False, stop)

            def halves(i):
                return slice(i * HALF, (i + 1) * HALF)

            class Convolution:

                def __init__(self, b, at=0):
                    self.b, self.at = b, at

                def more(self, n):
                    b = self.b
                    for i in range(self.at, min(self.at + n, GROUPS * CONV_MM)):
                        o, m = divmod(i, PAIR)
                        k, m = divmod(m, CONV_MM)
                        half, m = divmod(m, CONV_MM // KT)
                        tap, part = divmod(m, 3)
                        begin, end = m == 0 and k == 0, m == CONV_MM // KT - 1 and k == KT - 1
                        if m == 0 and half == 0 and o == 0:
                            pe.wait_ge(im_act, b * KT + k + 1)
                            pe.wait_ge(im_dve, b * KT + k + 1)
                        if begin:
                            pe.wait_ge(conv_out, (b + 1) * GROUPS + 2 * (o - 1) + half + 1)
                        tap = (TAP_ORDER if k == 0 else TAP_ORDER[::-1])[tap]
                        dy, dx = tap // 3 - 1, tap % 3 - 1
                        c0 = (k * TAPS + tap) * C + o * P
                        y0, y1 = max(half * H // 2, -dy), min((half + 1) * H // 2, H - dy)
                        to = cps[:, half].rearrange("p (h w) -> p h w", w=W)
                        ins = mm(to[:, y0 - half * H // 2:y1 - half * H // 2],
                                 (cw_hi, cw_hi, cw_lo)[part][:, c0:c0 + P],
                                 (im_hi, im_lo, im_hi)[part][:, k, y0 + dy:y1 + dy, 1 + dx:1 + dx + W], begin, end)
                        if end:
                            ins.then_inc(conv_pe, 1)
                        elif m == CONV_MM // KT - 1 and half == 1 and o == KT - 1:
                            ins.then_inc(im_free, 1)
                    self.at += n

            def keep_warm(n):
                for _ in range(n):
                    mm(cps[:, 0, 0:C_ALL], cst[:, C_ID:C_ID + P], cst[:, 0:C_ALL], True, True)

            class NoConvolution:
                at = 0

                def more(self, n):
                    pass

            def group_means(b, i):
                pe.wait_ge(gn_c[i], b * N_GN + GN_SENT)
                mm(slot[2][:, 0, 0:2 * KT], cst[:, C_GRP:C_GRP + P], mv[i][:].rearrange("p k s -> p (k s)"),
                   True, True).then_inc(gn_pe[i], 1)

            def project(to, c0, tile_ready=lambda k: None):
                for k in range(KT):
                    tile_ready(k)
                    for i in range(2):
                        last = split_mm(to[:, i], (w_hi[:, k, c0:c0 + P], w_lo[:, k, c0:c0 + P]),
                                        (xn_hi[:, k, halves(i)], xn_lo[:, k, halves(i)]), k == 0, k == KT - 1)
                last.then_inc(proj_pe, 1)

            def pooled_scores(b, i):
                h, t = divmod(i, MT)
                for half in range(2):
                    last = mm(slot[ST_SLOT[i]][:, half], ks[0:SM, h, t * P:(t + 1) * P], qs[0:SM, h, halves(half)],
                              True, True)
                last.then_inc(st_pe, 1)

            def by_head(s, lhsT, ready):
                for half in range(2):
                    for t in range(MT):
                        for h in range(HEADS):
                            last = mm(slot[s][HD * h:HD * (h + 1), half], lhsT(t, h), probs[:, h * MT + t, halves(half)],
                                      t == 0, t == MT - 1)
                    if ready is lden_pe or half == 1:
                        last.then_inc(ready, 1)

            def window_scores(b, to):
                for j in range(NW):
                    pe.wait_ge(prod_ready, b * NW + j + 1)
                    for half in range(2):
                        ins = mm(to[HD * j:HD * (j + 1), half], cst[:, C_HEAD:C_HEAD + HD], qk[:, j, halves(half)],
                                 True, True)
                ins.then_inc(ssum_pe, 1)

            def front(b, conv, first=False):
                starting = not first and isinstance(conv, NoConvolution)

                def tile_ready(k):
                    pe.wait_ge(xhi_ready, b * KT + k + 1)
                    pe.wait_ge(xlo_ready, b * KT + k + 1)

                project(slot[0], WLQ, tile_ready)
                if starting:
                    keep_warm(WARM[10])
                pe.wait_ge(pool_c, (b + 1) * N_POOL)
                if not first:
                    pe.wait_ge(y_ready, b * KT - 1)
                for k in range(KT):
                    split_mm(slot[1][:, 0, 0:G], (w_hi[:, k, WLK:WLK + P], w_lo[:, k, WLK:WLK + P]),
                             (pool_hi[:, k], pool_lo[:, k]), k == 0, k == KT - 1)
                for t in range(MT):
                    m = slice(t * P, (t + 1) * P)
                    for k in range(KT):
                        ins = split_mm(slot[1][:, 1, m], (pool_hi[:, k, m], pool_lo[:, k, m]),
                                       (w_hi[:, k, WLV:WLV + P], w_lo[:, k, WLV:WLV + P]), k == 0, k == KT - 1)
                ins.then_inc(proj_pe, 1)
                if not first:
                    pe.wait_ge(y_ready, b * KT)
                project(slot[2], WQ)
                pe.wait_ge(lq_dve, b + 1)
                project(slot[0], WK)
                conv.more(FRONT[0])
                if not first:
                    pe.wait_ge(qkv_sb, b * 3 + 1)
                    group_means(b - 1, 1)
                    pe.wait_ge(lk_act, (b + 1) * 2)
                    pe.wait_ge(lk_dve, b + 1)
                    project(slot[1], WV)
                conv.more(FRONT[1])
                for n in range(NB):
                    if n == 0:
                        pe.wait_ge(stacked, (b + 1) * STACK)
                        pe.wait_ge(qkv_sb, b * 3 + 2)
                    elif n == 1:
                        if first:
                            pe.wait_ge(lk_act, 2)
                            pe.wait_ge(lk_dve, 1)
                        else:
                            pe.wait_ge(qkv_sb, b * 3 + 3)
                    elif n == 2:
                        if not first:
                            pe.wait_ge(gn_c[1], (b - 1) * N_GN + GN_SENT + 1)
                    else:
                        pe.wait_ge(la_max, b * NB + n - 2)
                    for h in range(HEADS):
                        ins = mm(flat[LA_SLOT[n]][:, h * G:(h + 1) * G], qs[0:SC, h, n * P:(n + 1) * P], ks[0:SC, h],
                                 True, True)
                    ins.then_inc(la_pe, 1)
                    if first and n == 2:
                        project(cps, WV)
                    conv.more(FRONT[2 + n])
                    if starting:
                        keep_warm(WARM[1 + n])
                    if starting and n == NB - 1:
                        Convolution(b - 1).more(EARLY)
                if first:
                    pe.wait_ge(qkv_sb, 3)
                    window_scores(b, cps)
                pe.wait_ge(la_max, (b + 1) * NB)
                if first:
                    pe.wait_ge(zeroed, 1)
                nc.tensor.transpose(slot[2][:, 0, 0:P], l_max[:], cst[:, C_ID:C_ID + P]).then_inc(lmt_pe, 1)
                conv.more(FRONT[10])
                if not first:
                    window_scores(b, slot[0])
                conv.more(FRONT[11])
                pe.wait_ge(ssum_sb, b + 1)
                pe.wait_ge(lm_dve, (b + 1) * 2)
                for n in range(NB):
                    ins = nc.tensor.transpose(slot[2][:, n // 4, (n % 4) * P:(n % 4 + 1) * P],
                                              q_w[:, n * P:(n + 1) * P], cst[:, C_ID:C_ID + P])
                ins.then_inc(stok_pe, 1)
                if first:
                    pe.wait_ge(ones, 1)
                pe.wait_ge(max_stacked, (b + 1) * MAX_STACK)
                for i in range(2):
                    pooled_scores(b, i)
                conv.more(FRONT[12])
                if not (first or starting):
                    Convolution(b - 1).more(EARLY)

            def rest(b, first, last):
                conv = NoConvolution() if first else Convolution(b - 1, EARLY)
                conv.more(REST[0])
                for i in range(2, LT - NW):
                    pe.wait_ge(st_exp, b * LT + i - 1)
                    pooled_scores(b, i)
                    conv.more(REST[1])
                pe.wait_ge(soft_c, (b + 1) * N_SOFT)
                for n in range(NB):
                    ins = nc.tensor.transpose(slot[2][:, n // 4, (n % 4) * P:(n % 4 + 1) * P],
                                              s_soft[:, n].rearrange("p j h -> p (j h)"), cst[:, C_ID:C_ID + P])
                ins.then_inc(pt_pe, 1)
                conv.more(REST[2])
                pe.wait_ge(pt_act, b + 1)
                for j in range(NW):
                    if j < 2:
                        pe.wait_ge(st_exp, b * LT + j + 3)
                    elif j == 2:
                        if not last:
                            group_means(b + 1, 0)
                        pe.wait_ge(pv_ready, b * NW + 1)
                    elif not last:
                        pe.wait_ge(gn_c[0], (b + 1) * N_GN + GN_SENT + 1)
                    for half in range(2):
                        ins = mm(slot[PB_SLOT[j]][:, half], sel[:, j], p_w[:, halves(half)], True, True)
                    ins.then_inc(pb_pe, 1)
                    conv.more(REST[3])
                for i in range(LT - NW, LT):
                    if i < LT - 1:
                        pe.wait_ge(pv_ready, b * NW + i - 2)
                    else:
                        pe.wait_ge(st_exp, b * LT + 5)
                    pooled_scores(b, i)
                    conv.more(REST[4])
                pe.wait_ge(st_exp, (b + 1) * LT)
                by_head(2, lambda t, h: cst[:, C_ONE:C_ONE + HD], lden_pe)
                pe.wait_ge(pv_dve, (b + 1) * 2)
                for half in range(2):
                    ins = mm(slot[1][:, half], w_out[:, 0], q_w[:, halves(half)], True, True)
                ins.then_inc(out_pe, 1)
                by_head(0, lambda t, h: lv[:, t, HD * h:HD * (h + 1)], lpv_pe)
                conv.more(REST[5])
                if first:
                    keep_warm(WARM[9])
                pe.wait_ge(lnorm, b + 1)
                for half in range(2):
                    ins = mm(slot[2][:, half], w_out[:, 1], k_w[:, halves(half)], True, True)
                ins.then_inc(out_pe, 1)
                conv.more(PAIR - conv.at)
                return conv

            def step(b, first, last):
                conv = rest(b, first, last)
                if first:
                    pe.wait_ge(cw_split, 4 * KT)
                if not last:
                    front(b + 1, conv)
                else:
                    conv.more(CONV_MM // 2)
                    pe.wait_ge(y_ready, B * KT)
                    group_means(b, 1)
                    conv.more(PAIR)

            pe.wait_ge(cst_in, 16)
            group_means(0, 0)
            keep_warm(WARM[0])
            pe.wait_ge(w_split, 2)
            pe.wait_ge(gn_c[0], N_GN)
            front(0, NoConvolution(), first=True)
            step(0, True, False)
            with pe.Fori(1, B - 1) as b:
                step(b, False, False)
            step(B - 1, False, True)
            Convolution(B - 1).more(GROUPS * CONV_MM)


def constants():
    import numpy as np
    c, s = np.zeros((P, C_ALL), np.float32), np.zeros((P, SEL_COLS), np.float32)
    p = np.arange(P)
    c[:, C_ID:C_ID + P] = np.eye(P)
    c[:, C_GRP:C_GRP + P] = (p[:, None] // GROUP == p[None] // GROUP) / GROUP
    for h in range(HEADS):
        c[:, C_HEAD + h] = p // HD == h
    c[:, C_ONE:C_ONE + HD] = 1
    for j in range(NW):
        for part in range(2):
            s[:, j * P:(j + 1) * P] += p[:, None] == HD * j + HEADS * part + p[None] // HD
    c[:, C_IX:C_IX + H] = np.arange(1, H + 1)
    c[:, C_POS:C_POS + H] = np.linspace(-1, 1, H)
    return c, s


def kernel(x, L0_conv_h_qkv_w, L0_conv_h_proj_w, L0_conv_h_proj_b, L0_conv_l_q_w, L0_conv_l_kv_w, L0_conv_l_proj_w,
           L0_conv_l_proj_b, L1_conv_weight, L1_conv_bias, L1_conv_mask_weight, L1_conv_filter):
    import numpy as np
    import concourse.bacc as bacc
    from concourse.bass_utils import run_bass_kernel_spmd

    tiles = lambda a: np.ascontiguousarray(np.asarray(a).reshape(KT, P, -1))
    mixed = lambda a: np.asarray(a).reshape(C, HEADS, HD).transpose(0, 2, 1).reshape(C, P)
    cols = lambda a: np.ascontiguousarray(np.asarray(a).reshape(-1, P).T)
    arrays = {
        "x": np.ascontiguousarray(np.asarray(x).reshape(B, KT, P, HW)),
        "h_qkv": tiles(L0_conv_h_qkv_w), "l_q": tiles(mixed(L0_conv_l_q_w)),
        "l_kv": tiles(np.concatenate([mixed(L0_conv_l_kv_w[:, :P]), L0_conv_l_kv_w[:, P:]], 1)),
        "h_proj": np.ascontiguousarray(L0_conv_h_proj_w), "l_proj": np.ascontiguousarray(L0_conv_l_proj_w),
        "h_bias": cols(L0_conv_h_proj_b), "l_bias": cols(L0_conv_l_proj_b),
        "conv_w": tiles(np.asarray(L1_conv_weight).reshape(C, C, TAPS).transpose(1, 2, 0)),
        "conv_b": cols(L1_conv_bias), "mask_w": cols(L1_conv_mask_weight), "filt": cols(L1_conv_filter),
        "consts": constants()[0], "selectors": constants()[1],
    }
    nc = bacc.Bacc("TRN2", target_bir_lowering=False, num_devices=1)
    t = {n: nc.dram_tensor(n, a.shape, F32, kind="ExternalInput").ap() for n, a in arrays.items()}
    out = nc.dram_tensor("out", (B, KT, P, HW), F32, kind="ExternalOutput").ap()
    build(nc, t["x"], (t["h_qkv"], t["l_q"], t["l_kv"]), t["h_proj"], t["l_proj"], t["h_bias"], t["l_bias"],
          t["conv_w"], t["conv_b"], t["mask_w"], t["filt"], t["consts"], t["selectors"], out)
    r = run_bass_kernel_spmd(nc, [arrays], core_ids=[0])
    return np.asarray(r.results[0]["out"]).reshape(B, C, H, W)
```
